# Optimizing a Trainium2 kernel written in Bass

```python
import numpy as np
import jax
import jax.numpy as jnp

def _softmax(x, axis=-1):
    return jax.nn.softmax(x, axis=axis)

def _gelu(x):
    return jax.nn.gelu(x, approximate=True)

def _silu(x):
    return jax.nn.silu(x)

def _sigmoid(x):
    return jax.nn.sigmoid(x)

def _layernorm(x, axis=-1, eps=1e-05):
    m = jnp.mean(x, axis=axis, keepdims=True)
    v = jnp.var(x, axis=axis, keepdims=True)
    return (x - m) / jnp.sqrt(v + eps)

def _scatter_add(tgt, idx, src, axis=0):
    return tgt.at[idx].add(src)

def _segment_sum(src, seg, n):
    return jax.ops.segment_sum(src, seg, n)
kernel_name = 'mk_xattn_ffn_d4_seqx_r8_6f2d93'

def setup_inputs(seed: int=0):
    np.random.seed(seed)
    _w = jnp.asarray

    def _rec_inputs():
        import jax
        import jax.numpy as jnp
        _rk = jax.random.key(seed)
        x = -0.0002928 + 1 * jax.random.normal(jax.random.fold_in(_rk, 1), (1, 1024, 128), jnp.float32)
        _lenS = 1024 - jax.random.randint(jax.random.fold_in(_rk, 7), (1,), 0, max(1, 1024 // 4) + 1, jnp.int32)
        _lenS2 = 6404 - jax.random.randint(jax.random.fold_in(_rk, 8), (1,), 0, max(1, 6404 // 4) + 1, jnp.int32)
        _ctx_1024P = jax.random.normal(jax.random.fold_in(_rk, 11), (1, 16, 128), jnp.float32)
        _ctx_1024c = jax.random.dirichlet(jax.random.fold_in(_rk, 511), 0.3 * jnp.ones((16,), jnp.float32), (1, 6404))
        _ctx_1024t = jnp.einsum('bsk,bkd->bsd', _ctx_1024c, _ctx_1024P)
        _ctx_1024t = _ctx_1024t * jax.lax.rsqrt(jnp.mean(jnp.square(_ctx_1024t)) + 1e-12) * 0.953939
        ctx_1024 = -1.39393e-06 + 0.999914 * (_ctx_1024t + 0.3 * jax.random.normal(jax.random.fold_in(_rk, 611), (1, 6404, 128), jnp.float32))
        _validS = jnp.arange(1024)[None, :] < _lenS[:, None]
        _validS2 = jnp.arange(6404)[None, :] < _lenS2[:, None]
        _causal = jnp.tril(jnp.ones((1024, 1024), dtype=bool))
        mask_BxSxS2_bf1 = jnp.ones((1, 1024, 6404), dtype=bool)
        return (x, ctx_1024, mask_BxSxS2_bf1)
    x, ctx_1024, mask_BxSxS2_bf1 = _rec_inputs()

    def _L0_xattn_setup():
        import jax, jax.numpy as jnp
        import numpy as np
        B, S, D, H = (2, 256, 128, 16)
        DH = D // H

        def _split_heads(x):
            b, s, _ = x.shape
            return x.reshape(b, s, H, DH).transpose(0, 2, 1, 3)
        key = jax.random.key(seed)
        ks = jax.random.split(key, 12)
        scale = 1.0 / np.sqrt(D)
        inp = {'attn_from': jax.random.normal(ks[0], (B, S, D), jnp.float32), 'attn_to': jax.random.normal(ks[1], (B, S, D), jnp.float32), 'value': jax.random.normal(ks[2], (B, S, D), jnp.float32), 'mask': jnp.ones((B, S, S), dtype=bool), 'Wq': jax.random.normal(ks[3], (D, D), jnp.float32) * scale, 'bq': jnp.zeros((D,), jnp.float32), 'Wk': jax.random.normal(ks[4], (D, D), jnp.float32) * scale, 'bk': jnp.zeros((D,), jnp.float32), 'Wv': jax.random.normal(ks[5], (D, D), jnp.float32) * scale, 'bv': jnp.zeros((D,), jnp.float32), 'Wo': jax.random.normal(ks[6], (D, D), jnp.float32) * scale, 'bo': jnp.zeros((D,), jnp.float32)}
        return inp
    _L0_xattn_all = _L0_xattn_setup()
    _L0_xattn_in = {k: v for k, v in _L0_xattn_all.items() if k in ('Wq', 'bq', 'Wk', 'bk', 'Wv', 'bv', 'Wo', 'bo')}
    del _L0_xattn_all

    def _L0_ffn_setup():
        import jax, jax.numpy as jnp
        import numpy as np
        N_EMBD = 128
        N_EXP = 8
        TOP_K = 2
        CAPACITY = 512
        D_FF = 3 * N_EMBD
        key = jax.random.key(seed)
        k1, k2, k3, k4 = jax.random.split(key, 4)
        x = jax.random.normal(k1, (8, 256, N_EMBD), dtype=jnp.float32)
        w_gate = jax.random.normal(k2, (N_EMBD, N_EXP), dtype=jnp.float32) * 0.02
        c_fc = jax.random.normal(k3, (N_EXP, N_EMBD, D_FF), dtype=jnp.float32) * 0.02
        c_proj = jax.random.normal(k4, (N_EXP, D_FF // 2, N_EMBD), dtype=jnp.float32) * 0.02
        return {'x': x, 'w_gate': w_gate, 'c_fc': c_fc, 'c_proj': c_proj}
    _L0_ffn_all = _L0_ffn_setup()
    _L0_ffn_in = {k: v for k, v in _L0_ffn_all.items() if k in ('w_gate', 'c_fc', 'c_proj')}
    del _L0_ffn_all

    def _L1_xattn_setup():
        import jax, jax.numpy as jnp
        import numpy as np
        import math
        B, S, D, H = (4, 256, 128, 16)
        DH = D // H

        def _split_heads(x):
            b, s, _ = x.shape
            return x.reshape(b, s, H, DH).transpose(0, 2, 1, 3)
        key = jax.random.key(seed)
        ks = jax.random.split(key, 12)
        sc = 1.0 / math.sqrt(D)
        return {'x_q': jax.random.normal(ks[0], (B, S, D), jnp.float32), 'x_kv': jax.random.normal(ks[1], (B, S, D), jnp.float32), 'W_q': jax.random.normal(ks[2], (D, D), jnp.float32) * sc, 'b_q': jnp.zeros((D,), jnp.float32), 'W_k': jax.random.normal(ks[3], (D, D), jnp.float32) * sc, 'b_k': jnp.zeros((D,), jnp.float32), 'W_v': jax.random.normal(ks[4], (D, D), jnp.float32) * sc, 'b_v': jnp.zeros((D,), jnp.float32), 'W_out': jax.random.normal(ks[5], (D, D), jnp.float32) * sc, 'b_out': jnp.zeros((D,), jnp.float32)}
    _L1_xattn_all = _L1_xattn_setup()
    _L1_xattn_in = {k: v for k, v in _L1_xattn_all.items() if k in ('W_q', 'b_q', 'W_k', 'b_k', 'W_v', 'b_v', 'W_out', 'b_out')}
    del _L1_xattn_all

    def _L1_ffn_setup():
        import jax, jax.numpy as jnp
        import numpy as np
        EPS = 1e-09
        RMS_EPS = 1e-06
        TOP_K = 2
        LOOPS = 2

        def _rmsnorm(x, w):
            var = jnp.mean(x * x, axis=-1, keepdims=True)
            return x * jax.lax.rsqrt(var + RMS_EPS) * w

        def _swiglu(x, w1, w3, w2):
            h = jax.nn.silu(x @ w1) * (x @ w3)
            return h @ w2
        key = jax.random.key(seed)
        ks = jax.random.split(key, 5)
        B, S, D, F, E = (4, 256, 128, 256, 8)
        z = jax.random.normal(ks[0], (B, S, D), dtype=jnp.float32)
        norm_w = jnp.ones((D,), dtype=jnp.float32)
        router_w = jax.random.normal(ks[1], (D, E), dtype=jnp.float32) * 0.02
        w1 = jax.random.normal(ks[2], (E, D, F), dtype=jnp.float32) * 0.02
        w3 = jax.random.normal(ks[3], (E, D, F), dtype=jnp.float32) * 0.02
        w2 = jax.random.normal(ks[4], (E, F, D), dtype=jnp.float32) * 0.02
        return {'z': z, 'norm_w': norm_w, 'router_w': router_w, 'w1': w1, 'w3': w3, 'w2': w2}
    _L1_ffn_all = _L1_ffn_setup()
    _L1_ffn_in = {k: v for k, v in _L1_ffn_all.items() if k in ('norm_w', 'router_w', 'w1', 'w3', 'w2')}
    del _L1_ffn_all

    def _L2_xattn_setup():
        import jax, jax.numpy as jnp
        import numpy as np
        EMBED_DIM = 128
        NUM_HEADS = 16
        HEAD_DIM = EMBED_DIM // NUM_HEADS
        key = jax.random.key(seed)
        ks = jax.random.split(key, 7)
        B, S, E = (2, 256, EMBED_DIM)
        bound = float(np.sqrt(6.0 / (E + E)))
        mkw = lambda k: jax.random.uniform(k, (E, E), jnp.float32, -bound, bound)
        return {'query': jax.random.normal(ks[0], (B, S, E), jnp.float32), 'key': jax.random.normal(ks[1], (B, S, E), jnp.float32), 'value': jax.random.normal(ks[2], (B, S, E), jnp.float32), 'Wq': mkw(ks[3]), 'Wk': mkw(ks[4]), 'Wv': mkw(ks[5]), 'Wo': mkw(ks[6])}
    _L2_xattn_all = _L2_xattn_setup()
    _L2_xattn_in = {k: v for k, v in _L2_xattn_all.items() if k in ('Wq', 'Wk', 'Wv', 'Wo')}
    del _L2_xattn_all

    def _L2_ffn_setup():
        import jax, jax.numpy as jnp
        import numpy as np
        D_MODEL = 128
        N_EXPERTS = 8
        TOP_K = 2
        key = jax.random.key(seed)
        k1, k2, k3, k4 = jax.random.split(key, 4)
        B, S, D, E = (4, 256, D_MODEL, N_EXPERTS)
        dff = 4 * D
        lim = float(np.sqrt(6.0 / (D + dff)))
        return {'x': jax.random.normal(k1, (B, S, D), dtype=jnp.float32), 'router_w': jax.random.normal(k2, (D, E), dtype=jnp.float32) * (1.0 / np.sqrt(D)), 'router_b': jnp.zeros((E,), dtype=jnp.float32), 'expert_up': jax.random.uniform(k3, (E, dff, D), dtype=jnp.float32, minval=-lim, maxval=lim), 'expert_down': jax.random.uniform(k4, (E, D, dff), dtype=jnp.float32, minval=-lim, maxval=lim)}
    _L2_ffn_all = _L2_ffn_setup()
    _L2_ffn_in = {k: v for k, v in _L2_ffn_all.items() if k in ('router_w', 'router_b', 'expert_up', 'expert_down')}
    del _L2_ffn_all

    def _L3_xattn_setup():
        import jax, jax.numpy as jnp
        import numpy as np
        D_MODEL = 128
        N_HEADS = 16
        D_K = D_MODEL // N_HEADS
        B, S = (4, 256)

        def _xavier(key, out_dim, in_dim):
            limit = float(np.sqrt(6.0 / (in_dim + out_dim)))
            return jax.random.uniform(key, (out_dim, in_dim), jnp.float32, -limit, limit)
        key = jax.random.key(seed)
        ks = jax.random.split(key, 7)
        return {'query': jax.random.normal(ks[0], (B, S, D_MODEL), jnp.float32), 'key': jax.random.normal(ks[1], (B, S, D_MODEL), jnp.float32), 'value': jax.random.normal(ks[2], (B, S, D_MODEL), jnp.float32), 'W_q': _xavier(ks[3], D_MODEL, D_MODEL), 'b_q': jnp.zeros((D_MODEL,), jnp.float32), 'W_k': _xavier(ks[4], D_MODEL, D_MODEL), 'b_k': jnp.zeros((D_MODEL,), jnp.float32), 'W_v': _xavier(ks[5], D_MODEL, D_MODEL), 'b_v': jnp.zeros((D_MODEL,), jnp.float32), 'W_o': _xavier(ks[6], D_MODEL, D_MODEL), 'b_o': jnp.zeros((D_MODEL,), jnp.float32)}
    _L3_xattn_all = _L3_xattn_setup()
    _L3_xattn_in = {k: v for k, v in _L3_xattn_all.items() if k in ('W_q', 'b_q', 'W_k', 'b_k', 'W_v', 'b_v', 'W_o', 'b_o')}
    del _L3_xattn_all

    def _L3_ffn_setup():
        import jax, jax.numpy as jnp
        import numpy as np
        D, H, N, K = (128, 256, 8, 2)
        B, S = (4, 256)
        key = jax.random.key(seed)
        ks = jax.random.split(key, 4)
        x = jax.random.normal(ks[0], (B, S, D), dtype=jnp.float32)
        Wr = jax.random.normal(ks[1], (N, D), dtype=jnp.float32) / np.sqrt(D)
        br = jnp.zeros((N,), jnp.float32)
        Wl1 = jax.random.normal(ks[2], (N, D, 2 * H), dtype=jnp.float32) / np.sqrt(D)
        bl1 = jnp.zeros((N, 2 * H), jnp.float32)
        Wl2 = jax.random.normal(ks[3], (N, H, D), dtype=jnp.float32) / np.sqrt(H)
        bl2 = jnp.zeros((N, D), jnp.float32)
        biases_N = jnp.zeros((N,), jnp.float32)
        return {'x': x, 'Wr': Wr, 'br': br, 'Wl1': Wl1, 'bl1': bl1, 'Wl2': Wl2, 'bl2': bl2, 'biases_N': biases_N}
    _L3_ffn_all = _L3_ffn_setup()
    _L3_ffn_in = {k: v for k, v in _L3_ffn_all.items() if k in ('Wr', 'br', 'Wl1', 'bl1', 'Wl2', 'bl2', 'biases_N')}
    del _L3_ffn_all
    return {'x': x, 'ctx_1024': ctx_1024, 'mask_BxSxS2_bf1': mask_BxSxS2_bf1, 'L0_xattn_Wq': _L0_xattn_in['Wq'], 'L0_xattn_bq': _L0_xattn_in['bq'], 'L0_xattn_Wk': _L0_xattn_in['Wk'], 'L0_xattn_bk': _L0_xattn_in['bk'], 'L0_xattn_Wv': _L0_xattn_in['Wv'], 'L0_xattn_bv': _L0_xattn_in['bv'], 'L0_xattn_Wo': _L0_xattn_in['Wo'], 'L0_xattn_bo': _L0_xattn_in['bo'], 'L0_ffn_w_gate': _L0_ffn_in['w_gate'], 'L0_ffn_c_fc': _L0_ffn_in['c_fc'], 'L0_ffn_c_proj': _L0_ffn_in['c_proj'], 'L1_xattn_W_q': _L1_xattn_in['W_q'], 'L1_xattn_b_q': _L1_xattn_in['b_q'], 'L1_xattn_W_k': _L1_xattn_in['W_k'], 'L1_xattn_b_k': _L1_xattn_in['b_k'], 'L1_xattn_W_v': _L1_xattn_in['W_v'], 'L1_xattn_b_v': _L1_xattn_in['b_v'], 'L1_xattn_W_out': _L1_xattn_in['W_out'], 'L1_xattn_b_out': _L1_xattn_in['b_out'], 'L1_ffn_norm_w': _L1_ffn_in['norm_w'], 'L1_ffn_router_w': _L1_ffn_in['router_w'], 'L1_ffn_w1': _L1_ffn_in['w1'], 'L1_ffn_w3': _L1_ffn_in['w3'], 'L1_ffn_w2': _L1_ffn_in['w2'], 'L2_xattn_Wq': _L2_xattn_in['Wq'], 'L2_xattn_Wk': _L2_xattn_in['Wk'], 'L2_xattn_Wv': _L2_xattn_in['Wv'], 'L2_xattn_Wo': _L2_xattn_in['Wo'], 'L2_ffn_router_w': _L2_ffn_in['router_w'], 'L2_ffn_router_b': _L2_ffn_in['router_b'], 'L2_ffn_expert_up': _L2_ffn_in['expert_up'], 'L2_ffn_expert_down': _L2_ffn_in['expert_down'], 'L3_xattn_W_q': _L3_xattn_in['W_q'], 'L3_xattn_b_q': _L3_xattn_in['b_q'], 'L3_xattn_W_k': _L3_xattn_in['W_k'], 'L3_xattn_b_k': _L3_xattn_in['b_k'], 'L3_xattn_W_v': _L3_xattn_in['W_v'], 'L3_xattn_b_v': _L3_xattn_in['b_v'], 'L3_xattn_W_o': _L3_xattn_in['W_o'], 'L3_xattn_b_o': _L3_xattn_in['b_o'], 'L3_ffn_Wr': _L3_ffn_in['Wr'], 'L3_ffn_br': _L3_ffn_in['br'], 'L3_ffn_Wl1': _L3_ffn_in['Wl1'], 'L3_ffn_bl1': _L3_ffn_in['bl1'], 'L3_ffn_Wl2': _L3_ffn_in['Wl2'], 'L3_ffn_bl2': _L3_ffn_in['bl2'], 'L3_ffn_biases_N': _L3_ffn_in['biases_N']}

def reference(x, ctx_1024, mask_BxSxS2_bf1, L0_xattn_Wq, L0_xattn_bq, L0_xattn_Wk, L0_xattn_bk, L0_xattn_Wv, L0_xattn_bv, L0_xattn_Wo, L0_xattn_bo, L0_ffn_w_gate, L0_ffn_c_fc, L0_ffn_c_proj, L1_xattn_W_q, L1_xattn_b_q, L1_xattn_W_k, L1_xattn_b_k, L1_xattn_W_v, L1_xattn_b_v, L1_xattn_W_out, L1_xattn_b_out, L1_ffn_norm_w, L1_ffn_router_w, L1_ffn_w1, L1_ffn_w3, L1_ffn_w2, L2_xattn_Wq, L2_xattn_Wk, L2_xattn_Wv, L2_xattn_Wo, L2_ffn_router_w, L2_ffn_router_b, L2_ffn_expert_up, L2_ffn_expert_down, L3_xattn_W_q, L3_xattn_b_q, L3_xattn_W_k, L3_xattn_b_k, L3_xattn_W_v, L3_xattn_b_v, L3_xattn_W_o, L3_xattn_b_o, L3_ffn_Wr, L3_ffn_br, L3_ffn_Wl1, L3_ffn_bl1, L3_ffn_Wl2, L3_ffn_bl2, L3_ffn_biases_N):
    import jax
    import jax.numpy as jnp

    def _L0_xattn_ref(attn_from, attn_to, value, mask, Wq, bq, Wk, bk, Wv, bv, Wo, bo):
        import jax, jax.numpy as jnp
        import numpy as np
        B, S, D, H = (2, 256, 128, 16)
        DH = D // H

        def _split_heads(x):
            b, s, _ = x.shape
            return x.reshape(b, s, H, DH).transpose(0, 2, 1, 3)
        q = _split_heads(attn_from @ Wq.T + bq)
        k = _split_heads(attn_to @ Wk.T + bk)
        v = _split_heads(value @ Wv.T + bv)
        scores = jnp.einsum('bhqd,bhkd->bhqk', q, k) / jnp.sqrt(jnp.float32(DH))
        scores = jnp.where(mask[:, None, :, :], scores, jnp.float32(-1000000000.0))
        attn = jax.nn.softmax(scores, axis=-1)
        ctx = jnp.einsum('bhqk,bhkd->bhqd', attn, v)
        ctx = ctx.transpose(0, 2, 1, 3).reshape(ctx.shape[0], -1, H * DH)
        return ctx @ Wo.T + bo

    def _L0_ffn_ref(x, w_gate, c_fc, c_proj):
        import jax, jax.numpy as jnp
        import numpy as np
        N_EMBD = 128
        N_EXP = 8
        TOP_K = 2
        CAPACITY = 512
        D_FF = 3 * N_EMBD
        B, T, d = x.shape
        N = B * T
        xf = x.reshape(N, d)
        scores = jax.nn.softmax(xf @ w_gate, axis=-1)
        weights, idx = jax.lax.top_k(scores, TOP_K)
        flat_e = idx.reshape(-1)
        tok = jnp.repeat(jnp.arange(N), TOP_K)
        oh = jax.nn.one_hot(flat_e, N_EXP, dtype=jnp.int32)
        pos = (jnp.cumsum(oh, axis=0) * oh).sum(-1) - 1
        valid = pos < CAPACITY
        pos_c = jnp.where(valid, pos, 0)
        vmask = valid.astype(x.dtype)[:, None]
        exp_x = jnp.zeros((N_EXP, CAPACITY, d), x.dtype)
        exp_x = exp_x.at[flat_e, pos_c].add(xf[tok] * vmask)
        h = jnp.einsum('ecd,edf->ecf', exp_x, c_fc)
        a, g = jnp.split(h, 2, axis=-1)
        h = jax.nn.silu(a) * g
        exp_out = jnp.einsum('ecf,efd->ecd', h, c_proj)
        gathered = exp_out[flat_e, pos_c]
        w = weights.reshape(-1)[:, None] * vmask
        out = (gathered * w).reshape(N, TOP_K, d).sum(axis=1)
        return out.reshape(B, T, d)

    def _L1_xattn_ref(x_q, x_kv, W_q, b_q, W_k, b_k, W_v, b_v, W_out, b_out):
        import jax, jax.numpy as jnp
        import numpy as np
        import math
        B, S, D, H = (4, 256, 128, 16)
        DH = D // H

        def _split_heads(x):
            b, s, _ = x.shape
            return x.reshape(b, s, H, DH).transpose(0, 2, 1, 3)
        q = x_q @ W_q.T + b_q
        k = x_kv @ W_k.T + b_k
        v = x_kv @ W_v.T + b_v
        qh, kh, vh = (_split_heads(q), _split_heads(k), _split_heads(v))
        scale = 1.0 / math.sqrt(DH)
        scores = jnp.einsum('bhqd,bhkd->bhqk', qh, kh) * scale
        attn = jax.nn.softmax(scores, axis=-1)
        ctx = jnp.einsum('bhqk,bhkd->bhqd', attn, vh)
        ctx = ctx.transpose(0, 2, 1, 3).reshape(x_q.shape[0], x_q.shape[1], D)
        return ctx @ W_out.T + b_out

    def _L1_ffn_ref(z, norm_w, router_w, w1, w3, w2):
        import jax, jax.numpy as jnp
        import numpy as np
        EPS = 1e-09
        RMS_EPS = 1e-06
        TOP_K = 2
        LOOPS = 2

        def _rmsnorm(x, w):
            var = jnp.mean(x * x, axis=-1, keepdims=True)
            return x * jax.lax.rsqrt(var + RMS_EPS) * w

        def _swiglu(x, w1, w3, w2):
            h = jax.nn.silu(x @ w1) * (x @ w3)
            return h @ w2
        B, S, D = z.shape
        E = router_w.shape[-1]
        T = B * S
        for _ in range(LOOPS):
            z_norm = _rmsnorm(z, norm_w)
            logits = z_norm @ router_w
            scores = jax.nn.softmax(logits, axis=-1)
            topk_vals, topk_idx = jax.lax.top_k(scores, TOP_K)
            topk_vals = topk_vals / (jnp.sum(topk_vals, axis=-1, keepdims=True) + EPS)
            cw = jnp.sum(jax.nn.one_hot(topk_idx, E, dtype=z.dtype) * topk_vals[..., None], axis=-2)
            flat_z = z_norm.reshape(T, D)
            flat_cw = cw.reshape(T, E)
            mixed = jnp.zeros((T, D), dtype=z.dtype)
            for e in range(E):
                mixed = mixed + flat_cw[:, e:e + 1] * _swiglu(flat_z, w1[e], w3[e], w2[e])
            z = z + mixed.reshape(B, S, D)
        return z

    def _L2_xattn_ref(query, key, value, Wq, Wk, Wv, Wo):
        import jax, jax.numpy as jnp
        import numpy as np
        EMBED_DIM = 128
        NUM_HEADS = 16
        HEAD_DIM = EMBED_DIM // NUM_HEADS
        B, L, E = query.shape
        H, D = (NUM_HEADS, HEAD_DIM)
        scale = D ** (-0.5)
        q = (query @ Wq.T).reshape(B, L, H, D) * scale
        k = (key @ Wk.T).reshape(B, -1, H, D)
        v = (value @ Wv.T).reshape(B, -1, H, D)
        scores = jax.nn.sigmoid(jnp.einsum('blhd,bshd->bhls', q, k))
        o = jnp.einsum('bhls,bshd->blhd', scores, v).reshape(B, L, E)
        return o @ Wo.T

    def _L2_ffn_ref(x, router_w, router_b, expert_up, expert_down):
        import jax, jax.numpy as jnp
        import numpy as np
        D_MODEL = 128
        N_EXPERTS = 8
        TOP_K = 2
        B, S, D = x.shape
        E = expert_up.shape[0]
        x_flat = x.reshape(-1, D)
        logits = x_flat @ router_w + router_b
        probs = jax.nn.softmax(logits, axis=-1)
        top_w, top_idx = jax.lax.top_k(probs, TOP_K)
        comb = jnp.sum(top_w[..., None] * jax.nn.one_hot(top_idx, E, dtype=x.dtype), axis=1)
        output = jnp.zeros_like(x_flat)
        for e in range(E):
            h = jax.nn.gelu(x_flat @ expert_up[e].T, approximate=False)
            out_e = h @ expert_down[e].T
            output = output + comb[:, e:e + 1] * out_e
        return output.reshape(B, S, D)

    def _L3_xattn_ref(query, key, value, W_q, b_q, W_k, b_k, W_v, b_v, W_o, b_o):
        import jax, jax.numpy as jnp
        import numpy as np
        D_MODEL = 128
        N_HEADS = 16
        D_K = D_MODEL // N_HEADS
        B, S = (4, 256)

        def _xavier(key, out_dim, in_dim):
            limit = float(np.sqrt(6.0 / (in_dim + out_dim)))
            return jax.random.uniform(key, (out_dim, in_dim), jnp.float32, -limit, limit)
        b, sq, _ = query.shape
        sk = key.shape[1]
        Q = (query @ W_q.T + b_q).reshape(b, sq, N_HEADS, D_K).transpose(0, 2, 1, 3)
        K = (key @ W_k.T + b_k).reshape(b, sk, N_HEADS, D_K).transpose(0, 2, 1, 3)
        V = (value @ W_v.T + b_v).reshape(b, sk, N_HEADS, D_K).transpose(0, 2, 1, 3)
        scores = jnp.einsum('bhqd,bhkd->bhqk', Q, K) / jnp.sqrt(jnp.float32(D_K))
        attn = jax.nn.softmax(scores, axis=-1)
        out = jnp.einsum('bhqk,bhkd->bhqd', attn, V)
        out = out.transpose(0, 2, 1, 3).reshape(b, sq, D_MODEL)
        return out @ W_o.T + b_o

    def _L3_ffn_ref(x, Wr, br, Wl1, bl1, Wl2, bl2, biases_N):
        import jax, jax.numpy as jnp
        import numpy as np
        D, H, N, K = (128, 256, 8, 2)
        B, S = (4, 256)
        Bb, Ss, Dd = x.shape
        scores_BSN = jnp.einsum('bsd,nd->bsn', x, Wr) + br
        w_BSN = jax.nn.softmax(scores_BSN, axis=-1)
        _, idx_BSK = jax.lax.top_k(scores_BSN + biases_N[None, None, :], K)
        val_BSK = jnp.take_along_axis(w_BSN, idx_BSK, axis=-1)
        val_BSK = val_BSK / jnp.sum(val_BSK, axis=-1, keepdims=True)
        M = Bb * Ss
        x_MD = x.reshape(M, Dd)
        idx_MK = idx_BSK.reshape(M, K)
        val_MK = val_BSK.reshape(M, K)
        h_NM2H = jnp.einsum('md,ndh->nmh', x_MD, Wl1) + bl1[:, None, :]
        a_NMH, b_NMH = (h_NM2H[..., :H], h_NM2H[..., H:])
        y_NMD = jnp.einsum('nmh,nhd->nmd', jax.nn.silu(a_NMH) * b_NMH, Wl2) + bl2[:, None, :]
        ew_MN = jnp.zeros((M, N), x.dtype)
        ew_MN = ew_MN.at[jnp.arange(M)[:, None], idx_MK].set(val_MK)
        y_MD = jnp.einsum('mn,nmd->md', ew_MN, y_NMD)
        return y_MD.reshape(Bb, Ss, Dd)
    x = x + _L0_xattn_ref(_layernorm(x, axis=-1), ctx_1024, ctx_1024, mask_BxSxS2_bf1, L0_xattn_Wq, L0_xattn_bq, L0_xattn_Wk, L0_xattn_bk, L0_xattn_Wv, L0_xattn_bv, L0_xattn_Wo, L0_xattn_bo)
    x = x + _L0_ffn_ref(_layernorm(x, axis=-1), L0_ffn_w_gate, L0_ffn_c_fc, L0_ffn_c_proj)
    x = x + _L1_xattn_ref(_layernorm(x, axis=-1), ctx_1024, L1_xattn_W_q, L1_xattn_b_q, L1_xattn_W_k, L1_xattn_b_k, L1_xattn_W_v, L1_xattn_b_v, L1_xattn_W_out, L1_xattn_b_out)
    x = x + _L1_ffn_ref(_layernorm(x, axis=-1), L1_ffn_norm_w, L1_ffn_router_w, L1_ffn_w1, L1_ffn_w3, L1_ffn_w2)
    x = x + _L2_xattn_ref(_layernorm(x, axis=-1), ctx_1024, ctx_1024, L2_xattn_Wq, L2_xattn_Wk, L2_xattn_Wv, L2_xattn_Wo)
    x = x + _L2_ffn_ref(_layernorm(x, axis=-1), L2_ffn_router_w, L2_ffn_router_b, L2_ffn_expert_up, L2_ffn_expert_down)
    x = x + _L3_xattn_ref(_layernorm(x, axis=-1), ctx_1024, ctx_1024, L3_xattn_W_q, L3_xattn_b_q, L3_xattn_W_k, L3_xattn_b_k, L3_xattn_W_v, L3_xattn_b_v, L3_xattn_W_o, L3_xattn_b_o)
    x = x + _L3_ffn_ref(_layernorm(x, axis=-1), L3_ffn_Wr, L3_ffn_br, L3_ffn_Wl1, L3_ffn_bl1, L3_ffn_Wl2, L3_ffn_bl2, L3_ffn_biases_N)
    return x

_drawn_inputs = setup_inputs


def setup_inputs(seed=0):
    import zlib

    import numpy as np

    out = dict(_drawn_inputs(seed))
    spreads = {'L0_xattn_bq': (0.0, 0.8),
     'L0_xattn_bk': (0.0, 2.0),
     'L0_xattn_bv': (0.0, 0.288),
     'L0_xattn_bo': (0.0, 0.382),
     'L1_xattn_b_q': (0.0, 0.8),
     'L1_xattn_b_k': (0.0, 2.0),
     'L1_xattn_b_v': (0.0, 0.354),
     'L1_xattn_b_out': (0.0, 0.359),
     'L1_ffn_norm_w': (1.0, 0.6),
     'L2_ffn_router_b': (0.0, 2.0),
     'L3_xattn_b_q': (0.0, 2.0),
     'L3_xattn_b_k': (0.0, 2.0),
     'L3_xattn_b_v': (0.0, 2.0),
     'L3_xattn_b_o': (0.0, 2.0),
     'L3_ffn_br': (0.0, 2.0),
     'L3_ffn_bl1': (0.0, 2.0),
     'L3_ffn_bl2': (0.0, 2.0),
     'L3_ffn_biases_N': (0.0, 2.0)}
    factors = {'L0_ffn_w_gate': 8.0,
     'L0_ffn_c_fc': 8.0,
     'L0_ffn_c_proj': 8.0,
     'L1_ffn_router_w': 8.0,
     'L1_ffn_w1': 8.0,
     'L1_ffn_w3': 8.0,
     'L1_ffn_w2': 8.0,
     'L2_ffn_router_w': 8.0,
     'L2_ffn_expert_up': 22.344,
     'L2_ffn_expert_down': 8.0,
     'L3_xattn_W_q': 8.0,
     'L3_xattn_W_k': 8.0,
     'L3_xattn_W_v': 8.0,
     'L3_xattn_W_o': 8.0,
     'L3_ffn_Wr': 8.0,
     'L3_ffn_Wl1': 8.0,
     'L3_ffn_Wl2': 8.0}
    for name, (base, spread) in spreads.items():
        noise = np.random.default_rng([zlib.crc32(name.encode()), seed]).standard_normal(out[name].shape)
        drawn = base * np.exp(spread * noise) if base else spread * noise
        out[name] = jnp.asarray(drawn.astype(out[name].dtype))
    for name, factor in factors.items():
        out[name] = (out[name] * factor).astype(out[name].dtype)
    return out
```

```python
from contextlib import ExitStack

import concourse.bass as bass
from concourse import mybir

ALU = mybir.AluOpType
ACT = mybir.ActivationFunctionType
AX = mybir.AxisListType
F32 = mybir.dt.float32
F16 = mybir.dt.float16
U32 = mybir.dt.uint32
U16 = mybir.dt.uint16
U8 = mybir.dt.uint8
I32 = mybir.dt.int32

P = 128
D = 128
T = 1024
NT = T // P
KEYS = 6404
HEADS, DH = 16, 8
HG = 4
NG = HEADS // HG
ROWS = P // HG
QB = 512
NQB = T // QB
QT = QB // P
KT = -(-KEYS // P)
CH = 512
NCH = -(-KEYS // CH)
VC = DH + 1
M_ROW = 3 * DH
M_SCALE = 64.0
SCALE = float(DH) ** -0.5
E = 8
CAPACITY = 512
MASKED = 32768.0
M_LEAST = -16384.0
PIECES = 4
RING = 4
LAG = 2

FFN = [dict(fs=96, nk=2, gated=True, act=ACT.Silu, loops=1, alpha=1.0, beta=0.0),
       dict(fs=128, nk=2, gated=True, act=ACT.Silu, loops=2, alpha=1e-9, beta=1.0),
       dict(fs=128, nk=4, gated=False, act=ACT.Gelu, loops=1, alpha=1.0, beta=0.0),
       dict(fs=128, nk=2, gated=True, act=ACT.Silu, loops=1, alpha=0.0, beta=1.0)]


def keys_of(kt):
    return min(P, KEYS - kt * P)


def chunk_of(c):
    return min(CH, KEYS - c * CH)


class Count:

    def __init__(self, handle):
        self.handle, self.n = handle, 0

    def by(self, instruction, step=1):
        instruction.then_inc(self.handle, step)
        self.n += step
        return self.n


def build(nc, A, out):
    ctx = ExitStack()
    with ctx:
        def sb(name, shape, dt=F32):
            return ctx.enter_context(nc.sbuf_tensor(name, shape, dt))

        pe, act, dve, pool, sp = nc.tensor, nc.scalar, nc.vector, nc.gpsimd, nc.sync

        S = ctx.enter_context(nc.psum_tensor("scores", [P, 4, CH], F32))
        MX = ctx.enter_context(nc.psum_tensor("max_scores", [P, 2, CH], F32))
        AV = ctx.enter_context(nc.psum_tensor("av", [P, CH], F32))
        MISC = ctx.enter_context(nc.psum_tensor("misc", [P, CH], F32))

        ctxT = sb("ctxT", [P, KEYS])
        xs = sb("xs", [P, NT, D])
        xn = sb("xn", [P, NT, D])
        xnT = sb("xnT", [P, T])
        sq = sb("sq", [P, NT, D])
        stat = sb("stat", [P, 4, NT])
        KA = sb("KA", [P, KEYS], F16)
        KB = sb("KB", [P, KEYS], F16)
        V_all = sb("V_all", [P, KT, HEADS, VC])
        Vst = sb("Vst", [P, KT, HG, VC])
        Qst = sb("Qst", [P, NG, T], F16)
        QPa = sb("QPa", [P, HG, QB], F16)
        QPb = sb("QPb", [P, HG, QB], F16)
        prob = sb("prob", [P, RING, 2 * QB])
        kb32 = sb("kb32", [P, 2, CH])
        hi16 = sb("hi16", [P, 2, CH], F16)
        mpart = sb("mpart", [P, QT, HG, NCH])
        mm = sb("mm", [P, QT, HG])
        Mx = sb("Mx", [P, QT, HG, ROWS])
        oS = sb("oS", [P, QB])
        rden = sb("rden", [P, QT, HG])
        o_tok = sb("o_tok", [P, NT, D])
        cst = sb("cst", [P, 5])
        ident = sb("ident", [P, P])
        upper = sb("upper", [P, P])
        ones = sb("ones", [P, P])
        iota = sb("iota", [P, E])
        aw = [dict(q=sb(f"Wq{i}", [P, NG, P]), k=sb(f"Wk{i}", [P, NG, P]), v=sb(f"Wv{i}", [P, P]),
                   o=sb(f"Wo{i}", [P, P]), b=sb(f"bqk{i}", [P, 2, NG]), r=sb(f"bvo{i}", [P, 2, P]))
              for i in range(2)]
        WkCur = sb("WkCur", [P, P])
        bCur = sb("bCur", [P, 2])
        bq = sb("bq", [P, 2, 2, NG])
        Fin = sb("Fin", [P, E, 512])
        Fout = sb("Fout", [P, E, 4, D])
        FinCur = sb("FinCur", [P, 2, 512])
        Wg = sb("Wg", [P, E])
        rbias = sb("rbias", [P, 2, E])
        normw = sb("normw", [P, D])
        b1 = sb("b1", [P, E, 4])
        msum = sb("msum", [P, PIECES])
        mflag = sb("mflag", [P, 2])
        mcount = sb("mcount", [P, 1], I32)
        rowany = sb("rowany", [P, NT])
        vmean = sb("vmean", [P, D])
        bigI = sb("bigI", [P, P], F16)
        b1Cur = sb("b1Cur", [P, 2, 4])
        b2 = sb("b2", [E, D])
        hT = prob[:].rearrange("p r (k c) -> p (r k) c", c=CH).rearrange("p (a b) c -> p a b c", a=2)
        gA = kb32
        yacc = sq
        cwT = kb32[0:E].rearrange("p a c -> p (a c)")
        m8 = sq[:].rearrange("p t d -> p (t d)").bitcast(U8).rearrange("p (a r c) -> p a r c", a=4, r=2)
        m16 = xn[:].rearrange("p t d -> p (t d)").bitcast(F16).rearrange("p (a r c) -> p a r c", a=2, r=2)
        zs = o_tok
        lg = sb("lg", [P, NT, E])
        sel = sb("sel", [P, NT, E])
        top = sb("top", [P, NT, E])
        idx = sb("idx", [P, NT, E], U32)
        idf = sb("idf", [P, NT, E])
        msk = sb("msk", [P, NT, E])
        t1 = sb("t1", [P, NT, E])
        t2 = sb("t2", [P, NT, E])
        cum = sb("cum", [P, NT, E])
        cw = sb("cw", [P, NT, E])
        cwCur = sb("cwCur", [P, NT, 2])
        r1 = sb("r1", [P, 3, NT])

        names = ["seq", "score", "exp", "av", "mxs", "mxr", "kproj", "ksplit", "kstack", "qready", "miscfree",
                 "vstage", "wcur", "avout", "otr", "dvs", "mtr", "proj", "evac", "stack", "h", "hact", "hready",
                 "y", "yread", "cur", "mload0", "mload1", "mload2", "mload3", "mconv0", "mconv1", "msum"]
        handles = [ctx.enter_context(nc.semaphore("s_" + n)) for n in names]
        sem = {n: Count(h) for n, h in zip(names, handles)}
        cleared = range(min(h.num for h in handles), max(h.num for h in handles) + 1)
        assert len(cleared) == len(handles)
        d_const = Count(ctx.enter_context(nc.semaphore("d_const")))
        d_ctx = Count(ctx.enter_context(nc.semaphore("d_ctx")))
        d_attn = [Count(ctx.enter_context(nc.semaphore(f"d_attn{i}"))) for i in range(4)]
        d_ffn = [Count(ctx.enter_context(nc.semaphore(f"d_ffn{i}"))) for i in range(4)]
        d_out = Count(ctx.enter_context(nc.semaphore("d_out")))

        mask_n, mask_read = [0, 0], {}

        def barrier():
            nc.all_engine_barrier(sems_to_clear=cleared)
            for c in sem.values():
                c.n = 0
            mask_n[:] = [0, 0]
            mask_read.clear()

        def wait(eng, name, value=None):
            value = sem[name].n if value is None else value
            if value > 0:
                eng.wait_ge(sem[name].handle, value)

        def after(eng):
            wait(eng, "seq")
            return eng

        def step(instruction):
            sem["seq"].by(instruction)

        def load_attn(l):
            w = aw[l % 2]
            for dst, src in ((w["q"], A[f"Wq{l}"]), (w["k"], A[f"Wk{l}"]), (w["v"], A[f"Wv{l}"]),
                             (w["o"], A[f"Wo{l}"]), (w["b"], A[f"bqk{l}"])):
                d_attn[l].by(sp.dma_start(dst[:], src), 16)
            d_attn[l].by(sp.dma_start(w["r"][:], A[f"bvo{l}"].partition_broadcast(P)), 16)

        def load_ffn(l):
            f = FFN[l]
            nin = f["fs"] * f["nk"] * (2 if f["gated"] else 1)
            d_ffn[l].by(sp.dma_start(Fin[:, :, 0:nin], A[f"Fin{l}"]), 16)
            d_ffn[l].by(sp.dma_start(Fout[0:f["fs"], :, 0:f["nk"], :], A[f"Fout{l}"]), 16)
            d_ffn[l].by(sp.dma_start(Wg[:], A[f"Wg{l}"]), 16)
            if l == 1:
                d_ffn[l].by(sp.dma_start(normw[:], A["normw"].partition_broadcast(P)), 16)
            if l >= 2:
                d_ffn[l].by(sp.dma_start(rbias[:], A[f"rb{l}"].partition_broadcast(P)), 16)
            if l == 3:
                d_ffn[l].by(sp.dma_start(b1[:], A["b1"]), 16)
                d_ffn[l].by(sp.dma_start(b2[:], A["b2"]), 16)

        def loaded(eng, c):
            eng.wait_ge(c.handle, c.n)

        for dst, src in ((xs, A["x"].rearrange("(t p) d -> p t d", p=P)), (cst, A["cst"]),
                         (ident, A["ident"]), (upper, A["upper"]), (ones, A["ones"])):
            d_const.by(sp.dma_start(dst[:], src), 16)
        d_const.by(sp.dma_start(iota[:], A["iota"].partition_broadcast(P)), 16)
        load_attn(0)
        d_ctx.by(sp.dma_start(ctxT[:], A["ctxT"]), 16)
        gam, bet, gamQ, betQ, rowc = (cst[:, i:i + 1] for i in range(5))

        for buf in (QPa, QPb):
            pool.memset(buf[:], 0.0)
        pool.memset(Mx[:], 0.0)
        pool.memset(V_all[:, :, :, DH:VC], 1.0)
        pool.memset(Vst[:], 0.0)
        dve.memset(oS[:], 0.0)
        barrier()

        def broadcast(ap, shape):
            return ap.broadcast_to(shape)

        def norm(dst, src, eps, centre=True, weight=None):
            full = [P, NT, D]
            cur = src
            if centre:
                step(after(dve).tensor_reduce(stat[:, 0, :], src[:], AX.X, ALU.add))
                step(after(dve).tensor_scalar(stat[:, 1, :], stat[:, 0, :], 1.0 / D, None, ALU.mult))
                step(after(dve).tensor_tensor(dst[:], src[:], broadcast(stat[:, 1, :].unsqueeze(2), full), ALU.subtract))
                cur = dst
            step(after(dve).tensor_tensor(sq[:], cur[:], cur[:], ALU.mult))
            step(after(dve).tensor_reduce(stat[:, 2, :], sq[:], AX.X, ALU.add))
            step(after(dve).tensor_scalar(stat[:, 1, :], stat[:, 2, :], 1.0 / D, eps, ALU.mult, ALU.add))
            step(after(act).activation(stat[:, 2, :], stat[:, 1, :], ACT.Sqrt))
            step(after(dve).reciprocal(stat[:, 3, :], stat[:, 2, :]))
            step(after(dve).tensor_tensor(dst[:], cur[:], broadcast(stat[:, 3, :].unsqueeze(2), full), ALU.mult))
            if weight is not None:
                step(after(dve).tensor_tensor(dst[:], dst[:], broadcast(weight[:].unsqueeze(1), full), ALU.mult))

        def transpose_tiles(dst, tile_of):
            for b in range(NQB):
                after(pe)
                for t in range(QT):
                    last = pe.transpose(S[:, b, t * P:(t + 1) * P], tile_of(b * QT + t), ident[:])
                step(last)
            step(after(act).activation(dst[:, 0:CH], S[:, 0, :], ACT.Copy))
            step(after(dve).tensor_copy(dst[:, CH:T], S[:, 1, :]))

        def split_chunk(i, dst, w, lhsT, rhs, bias_b, bias_g, gamma, beta, psum, combine, free, ready):
            free(pe)
            sem["kproj"].by(pe.matmul(psum[:, 0:w], lhsT, rhs, start=True, stop=True))
            wait(act, "kproj")
            wait(act, "kstack", ready[0] + i - 1)
            act.activation(hi16[:, i % 2, 0:w], psum[:, 0:w], ACT.Identity, bias=bias_g, scale=gamma)
            ins = act.activation(kb32[:, i % 2, 0:w], psum[:, 0:w], ACT.Identity, bias=bias_b, scale=beta)
            sem["ksplit"].by(ins)
            wait(combine, "ksplit")
            sem["kstack"].by(combine.tensor_tensor(dst, kb32[:, i % 2, 0:w], hi16[:, i % 2, 0:w], ALU.add))

        def mask_tile(kind, src, n, w):
            i = mask_n[kind]
            mask_n[kind] += 1
            slot = i % 2
            load, conv = f"mload{2 * kind + slot}", f"mconv{kind}"
            wait(sp, conv, i - 1)
            sem[load].by(sp.dma_start(m8[0:n, kind, slot, 0:w], src), 16)
            wait(pool, load)
            wait(pool, *mask_read.get((kind, slot), ("seq", 0)))
            sem[conv].by(pool.tensor_scalar(m16[0:n, kind, slot, 0:w], m8[0:n, kind, slot, 0:w], 1.0, MASKED,
                                            ALU.subtract, ALU.mult))
            wait(pe, conv)
            return m16[0:n, kind, slot, 0:w]

        def read_by(kind, name):
            mask_read[kind, (mask_n[kind] - 1) % 2] = (name, sem[name].n)

        ITEMS = [(qt, c, h) for qt in range(QT) for c in range(NCH) for h in range(HG)]

        def max_product(i, K, QPn, qb, masked, tile):
            qt, c, h = ITEMS[i]
            w = chunk_of(c)
            if masked and h == 0:
                first = (qb * QT + qt) * P
                tile[0] = mask_tile(1, A["mask"][first:first + P, c * CH:c * CH + w], P, w)
            ins = pe.matmul(MX[:, i % 2, 0:w], QPn[:, h, qt * P:(qt + 1) * P], K[:, c * CH:c * CH + w],
                            start=True, stop=not masked)
            if masked:
                ins = pe.matmul(MX[:, i % 2, 0:w], bigI[:], tile[0], start=False, stop=True)
            sem["mxs"].by(ins)
            if masked:
                read_by(1, "mxs")
            wait(dve, "mxs")
            sem["mxr"].by(dve.tensor_reduce(mpart[:, qt, h, c:c + 1], MX[:, i % 2, 0:w], AX.X, ALU.max))

        def phase(l, probs, ready_q, K, QP, nxt, kprep, pending, store_o, ring, qb, masked):
            softmax = l != 2
            items = []
            if nxt is not None and softmax:
                items = ITEMS
            base_rd = sem["mxr"].n
            mtile = [None]
            done = 0
            group_done = {}

            def max_item(i):
                wait(pe, "mxr", base_rd + i - 1)
                if i == 0:
                    wait(pe, "qready", nxt[3])
                    wait(pe, "kstack", nxt[2])
                max_product(i, nxt[0], nxt[1], 1 - qb, masked, mtile)

            def prep_item(c):
                w = chunk_of(c)

                def free(eng):
                    wait(eng, "miscfree")
                    if c == 0:
                        wait(eng, "wcur")
                split_chunk(c, KB[:, c * CH:c * CH + w], w, WkCur[:], ctxT[:, c * CH:c * CH + w],
                            bCur[:, 0:1], bCur[:, 1:2], gam, bet, MISC, pool, free, (0,))
                wait(act, "ksplit")
                sem["miscfree"].by(act.activation(kdone[:], kdone[:], ACT.Copy))

            def scores(kt):
                n = keys_of(kt)
                if masked:
                    tile = mask_tile(0, A["maskT"][kt * P:kt * P + n, qb * QB:(qb + 1) * QB], n, QB)
                for half in range(2):
                    r = ring["n"]
                    ring["n"] += 1
                    wait(pe, "exp", r - 1)
                    if kt == 0 and half == 0:
                        wait(pe, "qready", ready_q)
                    for i in range(2):
                        ins = pe.matmul(S[0:n, 2 * (r % 2) + i, :], K[:, kt * P:kt * P + n],
                                        QP[:, 2 * half + i, :], start=True, stop=not masked)
                        if masked:
                            ins = pe.matmul(S[0:n, 2 * (r % 2) + i, :], bigI[0:n, 0:n], tile, start=False, stop=True)
                    sem["score"].by(ins)
                    if masked:
                        read_by(0, "score")
                    wait(act, "score")
                    wait(act, "av", ring["owner"][r % RING])
                    sem["exp"].by(act.activation(
                        probs[0:n, r % RING, :], S[0:n, 2 * (r % 2):2 * (r % 2) + 2, :].rearrange("p a b -> p (a b)"),
                        ACT.Exp if softmax else ACT.Sigmoid, scale=SCALE))
                    ring["owner"][r % RING] = 10 ** 9
                    group_done[2 * kt + half] = (sem["exp"].n, r)

            def attend(kt):
                n = keys_of(kt)
                wait(pe, "exp", group_done[2 * kt + 1][0])
                if kt == 0:
                    wait(pe, "avout")
                    wait(pe, "vstage")
                for h in range(HG):
                    slot = group_done[2 * kt + h // 2][1] % RING
                    ins = pe.matmul(AV[ROWS * h:ROWS * h + VC, :], Vst[0:n, kt, h, :],
                                    probs[0:n, slot, (h % 2) * QB:(h % 2) * QB + QB],
                                    start=kt == 0, stop=kt == KT - 1)
                sem["av"].by(ins)
                for half in range(2):
                    ring["owner"][group_done[2 * kt + half][1] % RING] = sem["av"].n

            for kt in range(KT + LAG):
                if kt >= LAG:
                    attend(kt - LAG)
                if kt < KT:
                    scores(kt)
                if kt == LAG - 1:
                    for p in pending:
                        p()
                    pending.clear()
                while done < len(items) and done * KT < len(items) * (kt + 1):
                    max_item(done)
                    done += 1
                if kprep and kt >= 3 and (kt - 3) % 3 == 0 and (kt - 3) // 3 < NCH:
                    prep_item((kt - 3) // 3)
                if kt == KT - 1 and items:
                    finish_max(nxt[1], masked)

            def output():
                wait(act, "av", av_end)
                wait(act, "otr")
                sem["avout"].by(act.activation(oS[:], AV[:], ACT.Copy))
                wait(pe, "avout")
                wait(pe, "miscfree")
                for qt in range(QT):
                    ins = pe.transpose(MISC[:, qt * P:(qt + 1) * P], oS[:, qt * P:(qt + 1) * P], ident[:])
                sem["otr"].by(ins)
                wait(dve, "otr")
                o = MISC[:].rearrange("p (q h c) -> p q h c", q=QT, h=HG)
                dst = store_o()
                if softmax:
                    if masked:
                        sem["dvs"].by(dve.tensor_scalar(rden[:], o[:, :, :, DH], 1e-30, None, ALU.max))
                        wait(dve, "dvs")
                        sem["dvs"].by(dve.reciprocal(rden[:], rden[:]))
                    else:
                        sem["dvs"].by(dve.reciprocal(rden[:], o[:, :, :, DH]))
                    wait(dve, "dvs")
                    sem["miscfree"].by(dve.tensor_tensor(dst, o[:, :, :, 0:DH],
                                                         broadcast(rden[:].unsqueeze(3), [P, QT, HG, DH]), ALU.mult))
                else:
                    sem["miscfree"].by(dve.tensor_copy(dst, o[:, :, :, 0:DH]))

            av_end = sem["av"].n
            pending.append(output)

        def finish_max(QPn, masked):
            wait(dve, "mxr")
            sem["dvs"].by(dve.tensor_reduce(mm[:], mpart[:], AX.X, ALU.max))
            wait(dve, "dvs")
            wait(dve, "mtr")
            if masked:
                sem["dvs"].by(dve.tensor_scalar(mm[:], mm[:], M_LEAST * M_SCALE, None, ALU.max))
                wait(dve, "dvs")
            sem["dvs"].by(dve.tensor_scalar(Mx[:, :, :, M_ROW], mm[:], -1.0 / M_SCALE, None, ALU.mult))
            wait(pe, "dvs")
            wait(pe, "miscfree")
            for qt in range(QT):
                ins = pe.transpose(MISC[:, qt * P:(qt + 1) * P], Mx[:, qt, :, :].rearrange("p h r -> p (h r)"), ident[:])
            sem["mtr"].by(ins)
            wait(dve, "mtr")
            wait(dve, "mxs")
            for h in range(HG):
                rows = slice(ROWS * h, ROWS * h + ROWS)
                sem["qready"].by(dve.tensor_tensor(QPn[rows, h, :], QPn[rows, h, :], MISC[rows, :], ALU.add))
            wait(dve, "qready")
            sem["miscfree"].by(dve.tensor_copy(r1[:, 0, 0:1], r1[:, 1, 0:1]))

        kdone = sb("kdone", [1, 1])
        step(dve.memset(kdone[:], 0.0))
        step(dve.memset(r1[:], 0.0))

        def fill(QPn, g, qb):
            flat = Qst[:].rearrange("p g t -> p (g t)")
            for h in range(HG):
                rows = slice(ROWS * h, ROWS * h + ROWS)
                sem["qready"].by(dve.tensor_copy(QPn[rows, h, :], flat[rows, bass.ds(g * T + qb * QB, QB)]))

        def stage_v(g):
            src = V_all[:].rearrange("p k h c -> p k (h c)")
            dst = Vst[:].rearrange("p k h c -> p k (h c)")
            w = HG * VC
            full = KT - 1
            pool.tensor_copy(dst[:, 0:full, :], src[:, 0:full, bass.ds(g * w, w)])
            n = keys_of(full)
            sem["vstage"].by(pool.tensor_copy(dst[0:n, full, :], src[0:n, full, bass.ds(g * w, w)]))

        def stage_w(l, g):
            flat = aw[l % 2]["k"][:].rearrange("p g c -> p (g c)")
            sem["wcur"].by(pool.tensor_copy(WkCur[:], flat[:, bass.ds(g * P, P)]))
            for j in range(2):
                sem["wcur"].by(pool.tensor_copy(bCur[:, j:j + 1], bq[:, 1, j, bass.ds(g, 1)]))

        def group(l, g, last, masked=False):
            softmax = l != 2
            ring = {"n": 0, "owner": [0] * RING}
            pending = []
            stage_v(g)
            if not last:
                stage_w(l, g + 1)
            fill(QPb, g, 1)
            q1 = sem["qready"].n

            def store(qb):
                def at():
                    return o_tok[:, qb * QT:(qb + 1) * QT, bass.ds(g * ROWS, ROWS)].rearrange("p q (h c) -> p q h c", h=HG)
                return at

            phase(l, prob, 0, KA, QPa, (KA, QPb, 0, q1), not last, pending, store(0), ring, 0, masked)
            ready = sem["qready"].n
            nxt = None
            if not last:
                wait(dve, "score")
                fill(QPa, g + 1, 0)
                nxt = (KB, QPa, NCH, sem["qready"].n)
            phase(l, prob, ready, KA, QPb, nxt, False, pending, store(1), ring, 1, masked)
            for p in pending:
                p()
            if not last:
                wait(dve, "score")
                wait(dve, "kstack")
                step(dve.tensor_copy(KA[:], KB[:]))
            barrier()

        def first_max(masked):
            tile = [None]
            for i in range(len(ITEMS)):
                if i == 0:
                    wait(pe, "qready")
                    wait(pe, "kstack")
                    wait(pe, "evac")
                wait(pe, "mxr", i - 1)
                max_product(i, KA, QPa, 0, masked, tile)
            finish_max(QPa, masked)

        def groups(l, masked):
            with nc.Fori(0, NG - 1) as g:
                group(l, g, False, masked)
            group(l, NG - 1, True, masked)

        def sum_mask():
            n = KEYS * T // P // 2 // PIECES
            assert n == KEYS and 257 * n < 1 << 24
            flat = A["mask"].rearrange("(p r) k -> p (r k)", p=P)
            for i in range(PIECES):
                buf = KB[:] if i % 2 else prob[:].rearrange("p r c -> p (r c)").bitcast(F16)[:, 0:n]
                wait(sp, "msum", i - 1)
                load = sem[f"mload{i % 2}"]
                load.by(sp.dma_start(buf.bitcast(U8), flat[:, 2 * i * n:2 * (i + 1) * n]), 16)
                wait(act, f"mload{i % 2}")
                sem["msum"].by(act.activation(buf.bitcast(U16), buf.bitcast(U16), ACT.Copy,
                                              accum_out=msum[:, i:i + 1]))
            wait(dve, "msum")
            sem["dvs"].by(dve.tensor_reduce(mflag[:, 0:1], msum[:], AX.X, ALU.min))
            wait(dve, "dvs")
            sem["dvs"].by(dve.tensor_scalar(mflag[:, 1:2], mflag[:, 0:1], 257.0 * n, None, ALU.is_ge))
            wait(pe, "dvs")
            sem["msum"].by(pe.matmul(MISC[:, 0:1], ones[:], mflag[:, 1:2], start=True, stop=True))
            wait(dve, "msum")
            sem["miscfree"].by(dve.tensor_copy(mcount[:], MISC[:, 0:1]))

        def masked_groups():
            step(after(dve).tensor_scalar(bigI[:], ident[:], MASKED, None, ALU.mult))
            fill(QPa, 0, 0)
            for t in range(NT):
                u8 = KB[:].bitcast(U8)[:, 0:KEYS]
                wait(sp, "msum", t)
                sem["mload0"].by(sp.dma_start(u8, A["mask"][t * P:(t + 1) * P, :]), 16)
                wait(dve, "mload0")
                sem["msum"].by(dve.tensor_reduce(rowany[:, t:t + 1], u8, AX.X, ALU.max))
            barrier()
            first_max(True)
            barrier()
            groups(0, True)
            for kt in range(KT):
                n = keys_of(kt)
                last = pe.matmul(MISC[:, 0:HEADS * VC], ones[0:n, :], V_all[0:n, kt, :, :].rearrange("p h c -> p (h c)"),
                                 start=kt == 0, stop=kt == KT - 1)
            step(last)
            mean = MISC[:, 0:HEADS * VC].rearrange("p (h c) -> p h c", h=HEADS)[:, :, 0:DH]
            step(after(dve).tensor_scalar(vmean[:].rearrange("p (h c) -> p h c", h=HEADS), mean, 1.0 / KEYS, None, ALU.mult))
            step(after(dve).tensor_scalar(rowany[:], rowany[:], -1.0, 1.0, ALU.mult, ALU.add))
            for t in range(NT):
                step(after(dve).scalar_tensor_tensor(o_tok[:, t, :], vmean[:], rowany[:, t:t + 1], o_tok[:, t, :],
                                                     ALU.mult, ALU.add))
            barrier()

        def attention(l):
            w = aw[l % 2]
            norm(xn, xs, 1e-5)
            transpose_tiles(xnT, lambda t: xn[:, t, :])
            loaded(dve, d_attn[l])
            for side, const, factors in ((0, 0.0, (betQ, gamQ)), (1, rowc, (bet, gam))):
                for j, factor in enumerate(factors):
                    step(after(dve).tensor_scalar(bq[:, side, j, :], w["b"][:, side, :], const, factor, ALU.add, ALU.mult))
            for eng in (pe, act, dve, pool):
                loaded(eng, d_attn[l])
                loaded(eng, d_ctx)
            barrier()

            def run(i, dst, n, lhsT, rhs, side, g):
                def free(eng):
                    wait(eng, "ksplit", i - 3)
                split_chunk(i, dst, n, lhsT, rhs, bq[:, side, 0, g:g + 1], bq[:, side, 1, g:g + 1],
                            gam if side else gamQ, bet if side else betQ, S[:, i % 4, :], dve, free, (0,))

            i = 0
            for g in range(NG):
                for qb in range(NQB):
                    run(i, Qst[:, g, qb * QB:(qb + 1) * QB], QB, w["q"][:, g, :], xnT[:, qb * QB:(qb + 1) * QB], 0, g)
                    i += 1
            for c in range(NCH):
                n = chunk_of(c)
                run(i, KA[:, c * CH:c * CH + n], n, w["k"][:, 0, :], ctxT[:, c * CH:c * CH + n], 1, 0)
                i += 1
            for j in range(-(-KT // 4)):
                tiles = range(4 * j, min(4 * j + 4, KT))
                wait(pe, "evac", j - 1)
                for kt in tiles:
                    n = keys_of(kt)
                    ins = pe.matmul(MX[0:n, j % 2, (kt % 4) * P:(kt % 4) * P + P], ctxT[:, kt * P:kt * P + n],
                                    w["v"][:], start=True, stop=True)
                sem["proj"].by(ins)
                wait(dve, "proj")
                parts = [(P, [t for t in tiles if keys_of(t) == P]), (keys_of(KT - 1), [t for t in tiles if keys_of(t) < P])]
                for n, ts in parts:
                    if not ts:
                        continue
                    k = len(ts)
                    a = ts[0]
                    src = MX[0:n, j % 2, (a % 4) * P:(a % 4 + k) * P].rearrange("p (k h c) -> p k h c", k=k, h=HEADS)
                    for q in range(k):
                        last = dve.tensor_tensor(V_all[0:n, a + q, :, 0:DH], src[:, q, :, :],
                                                 w["r"][0:n, 0, :].rearrange("p (h c) -> p h c", h=HEADS), ALU.add)
                sem["evac"].by(last)
            for t in range(QT):
                last = pe.matmul(AV[:, t * P:(t + 1) * P], zeros[:], zeros[:], start=True, stop=True)
            sem["proj"].by(last)
            wait(dve, "kstack")
            fill(QPa, 0, 0)
            if l == 0:
                sum_mask()
            if l != 2:
                first_max(False)
            barrier()
            if l == 0:
                n = nc.values_load(mcount[0:1, 0:1], min_val=0, max_val=P)
                with nc.If(n == P):
                    groups(l, False)
                with nc.Else():
                    masked_groups()
            else:
                groups(l, False)
            transpose_tiles(xnT, lambda t: o_tok[:, t, :])
            for b in range(NQB):
                after(pe)
                for t in range(QT):
                    tt = b * QT + t
                    last = pe.matmul(MX[:, b, t * P:(t + 1) * P], xnT[:, tt * P:(tt + 1) * P], w["o"][:],
                                     start=True, stop=True)
                step(last)
            for b in range(NQB):
                src = MX[:, b, :].rearrange("p (t d) -> p t d", d=D)
                part = xs[:, b * QT:(b + 1) * QT, :]
                step(after(dve).tensor_tensor(part, part, src, ALU.add))
            step(after(dve).tensor_tensor(xs[:], xs[:], broadcast(w["r"][:, 1, :].unsqueeze(1), [P, NT, D]), ALU.add))
            barrier()

        def route(l):
            f = FFN[l]
            full = [P, NT, E]
            L = MISC[:, 0:NT * E].rearrange("p (t e) -> p t e", e=E)
            after(pe)
            for t in range(NT):
                last = pe.matmul(L[:, t, :], xnT[:, t * P:(t + 1) * P], Wg[:], start=True, stop=True)
            step(last)
            if l >= 2:
                step(after(dve).tensor_tensor(lg[:], L, broadcast(rbias[:, 0, :].unsqueeze(1), full), ALU.add))
            else:
                step(after(dve).tensor_copy(lg[:], L))
            by = lg
            if l == 3:
                step(after(dve).tensor_tensor(sel[:], lg[:], broadcast(rbias[:, 1, :].unsqueeze(1), full), ALU.add))
                by = sel
            after(dve)
            for t in range(NT):
                last = dve.max(top[:, t, :], by[:, t, :])
            step(last)
            after(dve)
            for t in range(NT):
                last = dve.max_index(idx[:, t, :], top[:, t, :], by[:, t, :])
            step(last)
            step(after(dve).tensor_copy(idf[:, :, 0:2], idx[:, :, 0:2]))
            io = broadcast(iota[:].unsqueeze(1), full)
            step(after(dve).tensor_tensor(msk[:], io, broadcast(idf[:, :, 0:1], full), ALU.is_equal))
            step(after(dve).tensor_tensor(t1[:], io, broadcast(idf[:, :, 1:2], full), ALU.is_equal))
            step(after(dve).tensor_tensor(msk[:], msk[:], t1[:], ALU.add))
            step(after(dve).tensor_reduce(r1[:, 0, :], lg[:], AX.X, ALU.max))
            step(after(dve).tensor_tensor(t1[:], lg[:], broadcast(r1[:, 0, :].unsqueeze(2), full), ALU.subtract))
            step(after(act).activation(t2[:], t1[:], ACT.Exp))
            step(after(dve).tensor_reduce(r1[:, 1, :], t2[:], AX.X, ALU.add))
            step(after(dve).tensor_tensor(t1[:], t2[:], msk[:], ALU.mult))
            step(after(dve).tensor_reduce(r1[:, 2, :], t1[:], AX.X, ALU.add))
            step(after(dve).tensor_scalar(r1[:, 1, :], r1[:, 1, :], f["alpha"], None, ALU.mult))
            step(after(dve).scalar_tensor_tensor(r1[:, 0, :], r1[:, 2, :], f["beta"], r1[:, 1, :], ALU.mult, ALU.add))
            step(after(dve).reciprocal(r1[:, 1, :], r1[:, 0, :]))
            if l == 0:
                step(after(dve).memset(cum[:, 0, :], 0.0))
                for t in range(NT - 1):
                    step(after(dve).tensor_tensor(cum[:, t + 1, :], cum[:, t, :], msk[:, t, :], ALU.add))
                flat = [a[:].rearrange("p t e -> p (t e)") for a in (msk, cum)]
                after(pe)
                pe.matmul(MISC[:, 0:NT * E], upper[:], flat[0], start=True, stop=False)
                step(pe.matmul(MISC[:, 0:NT * E], ones[:], flat[1], start=False, stop=True))
                step(after(dve).tensor_scalar(t2[:], L, float(CAPACITY), None, ALU.is_lt))
                step(after(dve).tensor_tensor(t1[:], t1[:], t2[:], ALU.mult))
            step(after(dve).tensor_tensor(cw[:], t1[:], broadcast(r1[:, 1, :].unsqueeze(2), full), ALU.mult))

        def experts(l, pair):
            f = FFN[l]
            fs, nk, gated = f["fs"], f["nk"], f["gated"]
            nin = fs * nk * (2 if gated else 1)
            flat = Fin[:].rearrange("p e c -> p (e c)")
            for k in range(2):
                sem["cur"].by(dve.tensor_copy(FinCur[:, k, 0:nin], flat[:, bass.ds(pair * 1024 + k * 512, nin)]))
            sem["cur"].by(dve.tensor_copy(cwCur[:], cw[:, :, bass.ds(pair * 2, 2)]))
            if l == 3:
                b1f = b1[:].rearrange("p e c -> p (e c)")
                sem["cur"].by(dve.tensor_copy(b1Cur[:].rearrange("p a b -> p (a b)"), b1f[:, bass.ds(pair * 8, 8)]))
            wait(pe, "cur")
            wait(act, "cur")
            outf = Fout[:].rearrange("p e k d -> p (e k d)")
            todo = []
            n_act = 0

            def finish(unit, k, b, hbuf):
                bank = MX[:, unit % 2, :]
                wait(pe, "hready")
                wait(pe, "yread", QT * (unit - 1))
                for t in range(QT):
                    for j in range(nk):
                        ins = pe.matmul(bank[:, t * P:(t + 1) * P], hT[0:fs, hbuf, j, t * P:(t + 1) * P],
                                        outf[0:fs, bass.ds(pair * 2 * 4 * D + (k * 4 + j) * D, D)],
                                        start=j == 0, stop=j == nk - 1)
                sem["y"].by(ins)
                wait(dve, "y")
                for t in range(QT):
                    tt = b * QT + t
                    wait(dve, "yread", sem["yread"].n - QT)
                    sem["yread"].by(dve.scalar_tensor_tensor(yacc[:, tt, :], bank[:, t * P:(t + 1) * P],
                                                             cwCur[:, tt, k:k + 1], yacc[:, tt, :], ALU.mult, ALU.add))

            unit = 0
            for k in range(2):
                for b in range(NQB):
                    hb = unit % 2
                    tok = slice(b * CH, (b + 1) * CH)
                    for j in range(nk):
                        sides = ([j, nk + j] if gated else [j])
                        q = n_act % 2
                        wait(pe, "hready", n_act - 1)
                        for s, col in enumerate(sides):
                            ins = pe.matmul(S[0:fs, 2 * q + s, :], FinCur[:, k, col * fs:(col + 1) * fs], xnT[:, tok],
                                            start=True, stop=True)
                        sem["h"].by(ins)
                        wait(act, "h")
                        wait(act, "y", unit - 1)
                        bias = b1Cur[:, k, j:j + 1] if l == 3 else 0.0
                        if gated:
                            wait(act, "hready", n_act - 1)
                            sem["hact"].by(act.activation(gA[0:fs, q, :], S[0:fs, 2 * q, :], f["act"], bias=bias))
                            wait(dve, "hact")
                            if l == 3:
                                ins = dve.scalar_tensor_tensor(hT[0:fs, hb, j, :], S[0:fs, 2 * q + 1, :],
                                                               b1Cur[:, k, nk + j:nk + j + 1], gA[0:fs, q, :],
                                                               ALU.add, ALU.mult)
                            else:
                                ins = dve.tensor_tensor(hT[0:fs, hb, j, :], S[0:fs, 2 * q + 1, :], gA[0:fs, q, :],
                                                        ALU.mult)
                        else:
                            ins = act.activation(hT[0:fs, hb, j, :], S[0:fs, 2 * q, :], f["act"])
                        sem["hready"].by(ins)
                        n_act += 1
                    if todo:
                        todo.pop(0)()
                    ready = sem["hready"].n

                    def later(unit=unit, k=k, b=b, hb=hb):
                        finish(unit, k, b, hb)
                    todo.append(later)
                    unit += 1
            for x in todo:
                x()
            barrier()

        def ffn(l):
            f = FFN[l]
            for eng in (pe, dve, act, pool):
                loaded(eng, d_ffn[l])
            state = xs
            norm(xn, xs, 1e-5)
            if l == 1:
                state = zs
                step(after(dve).tensor_copy(zs[:], xn[:]))
            for loop in range(f["loops"]):
                if l == 1:
                    norm(xn, zs, 1e-6, centre=False, weight=normw)
                transpose_tiles(xnT, lambda t: xn[:, t, :])
                route(l)
                if l == 3:
                    for b in range(NQB):
                        after(pe)
                        for t in range(QT):
                            last = pe.transpose(S[0:E, b, t * P:(t + 1) * P], cw[:, b * QT + t, :], ident[:])
                        step(last)
                        step(after(dve).tensor_copy(cwT[:, b * CH:(b + 1) * CH], S[0:E, b, :]))
                    for b in range(NQB):
                        after(pe)
                        for t in range(QT):
                            tt = b * QT + t
                            last = pe.matmul(S[:, b, t * P:(t + 1) * P], cwT[:, tt * P:(tt + 1) * P], b2[:],
                                             start=True, stop=True)
                        step(last)
                        step(after(dve).tensor_copy(yacc[:, b * QT:(b + 1) * QT, :],
                                                    S[:, b, :].rearrange("p (t d) -> p t d", d=D)))
                else:
                    step(after(dve).memset(yacc[:], 0.0))
                barrier()
                with nc.Fori(0, E // 2) as pair:
                    experts(l, pair)
                step(after(dve).tensor_tensor(state[:], state[:], yacc[:], ALU.add))
            if l == 1:
                step(after(dve).tensor_tensor(xs[:], xs[:], zs[:], ALU.add))

        zeros = sb("zeros", [P, P])
        pool.memset(zeros[:], 0.0)
        for eng in (pe, act, dve, pool):
            loaded(eng, d_const)
        barrier()
        for l in range(4):
            load_ffn(l)
            if l < 3:
                load_attn(l + 1)
            attention(l)
            ffn(l)
            barrier()
        d_out.by(sp.dma_start(out.rearrange("(t p) d -> p t d", p=P), xs[:]), 16)
        loaded(sp, d_out)


def _layout(i):
    import numpy as np
    f = np.float32
    a = {}
    a["x"] = np.asarray(i["x"])[0]
    a["mask"] = np.asarray(i["mask_BxSxS2_bf1"])[0].view(np.uint8)
    a["maskT"] = a["mask"].T
    a["ctxT"] = np.asarray(i["ctx_1024"])[0].T

    names = [("L0_xattn_", "Wq bq Wk bk Wv bv Wo bo"), ("L1_xattn_", "W_q b_q W_k b_k W_v b_v W_out b_out"),
             ("L2_xattn_", "Wq - Wk - Wv - Wo -"), ("L3_xattn_", "W_q b_q W_k b_k W_v b_v W_o b_o")]

    def stack(w):
        s = np.zeros((D, NG, HG, 4, DH), f)
        s[:, :, :, 0:3, :] = w.reshape(D, NG, HG, 1, DH)
        return s.reshape(D, NG, P)

    for l, (pre, ns) in enumerate(names):
        wq, bq, wk, bk, wv, bv, wo, bo = (np.zeros(D, f) if n == "-" else np.asarray(i[pre + n]) for n in ns.split())
        a[f"Wq{l}"], a[f"Wk{l}"] = stack(wq.T), stack(wk.T)
        a[f"Wv{l}"], a[f"Wo{l}"] = wv.T, wo.T
        b = np.stack([stack(np.broadcast_to(x, (D, D)))[0] for x in (bq, bk)])
        a[f"bqk{l}"] = b.transpose(2, 0, 1)
        a[f"bvo{l}"] = np.stack([bv, bo])
    n = {k: np.asarray(v) for k, v in i.items() if "ffn" in k}
    a["Fin0"] = n["L0_ffn_c_fc"].transpose(1, 0, 2)
    a["Fout0"] = n["L0_ffn_c_proj"].reshape(E, 2, 96, D).transpose(2, 0, 1, 3)
    a["Wg0"] = n["L0_ffn_w_gate"]
    a["Fin1"] = np.concatenate([n["L1_ffn_w1"], n["L1_ffn_w3"]], axis=2).transpose(1, 0, 2)
    a["Fout1"] = n["L1_ffn_w2"].reshape(E, 2, P, D).transpose(2, 0, 1, 3)
    a["Wg1"] = n["L1_ffn_router_w"]
    a["normw"] = n["L1_ffn_norm_w"]
    a["Fin2"] = n["L2_ffn_expert_up"].transpose(2, 0, 1)
    a["Fout2"] = n["L2_ffn_expert_down"].transpose(0, 2, 1).reshape(E, 4, P, D).transpose(2, 0, 1, 3)
    a["Wg2"] = n["L2_ffn_router_w"]
    a["rb2"] = np.stack([n["L2_ffn_router_b"], np.zeros(E, f)])
    a["Fin3"] = n["L3_ffn_Wl1"].transpose(1, 0, 2)
    a["Fout3"] = n["L3_ffn_Wl2"].reshape(E, 2, P, D).transpose(2, 0, 1, 3)
    a["Wg3"] = n["L3_ffn_Wr"].T
    a["rb3"] = np.stack([n["L3_ffn_br"], n["L3_ffn_biases_N"]])
    a["b1"] = n["L3_ffn_bl1"].reshape(E, 4, P).transpose(2, 0, 1)
    a["b2"] = n["L3_ffn_bl2"]
    r = np.arange(P) % ROWS
    lo_k, lo_q = (r >= 2 * DH) & (r < 3 * DH), (r >= DH) & (r < 2 * DH)
    a["cst"] = np.stack([np.where(lo_k, -1, 1), lo_k, np.where(lo_q, -1, 1), lo_q, M_SCALE * (r == M_ROW)], 1).astype(f)
    a["ident"] = np.eye(P, dtype=f)
    a["upper"] = np.triu(np.ones((P, P), f), 1)
    a["ones"] = np.ones((P, P), f)
    a["iota"] = np.arange(E, dtype=f)
    return {k: np.ascontiguousarray(v) for k, v in a.items()}


def kernel(**inputs):
    import concourse.bacc as _bacc
    from concourse import mybir as _mybir
    from concourse.bass_utils import run_bass_kernel_spmd as _run

    nc = _bacc.Bacc("TRN2", target_bir_lowering=False, num_devices=1)
    arrays, args = {}, {}
    for name, a in _layout(inputs).items():
        arrays[f"in_{name}"] = a
        args[name] = nc.dram_tensor(f"in_{name}", a.shape, _mybir.dt.from_np(a.dtype), kind="ExternalInput").ap()
    out = nc.dram_tensor("out_x", (T, D), _mybir.dt.from_np(arrays["in_x"].dtype), kind="ExternalOutput").ap()
    build(nc, args, out)
    r = _run(nc, [arrays], core_ids=[0])
    return r.results[0]["out_x"].reshape(1, T, D)
```

```python
from contextlib import ExitStack

import concourse.bass as bass
from concourse import mybir

ALU = mybir.AluOpType
ACT = mybir.ActivationFunctionType
AX = mybir.AxisListType
F32 = mybir.dt.float32
F16 = mybir.dt.float16
U32 = mybir.dt.uint32
U16 = mybir.dt.uint16
U8 = mybir.dt.uint8
I32 = mybir.dt.int32

P = 128
D = 128
T = 1024
NT = T // P
KEYS = 6404
HEADS, DH = 16, 8
HG = 4
NG = HEADS // HG
ROWS = P // HG
QB = 512
NQB = T // QB
QT = QB // P
KT = -(-KEYS // P)
CH = 512
NCH = -(-KEYS // CH)
VC = DH + 1
M_ROW = 3 * DH
M_SCALE = 64.0
SCALE = float(DH) ** -0.5
E = 8
EU = 4
CAPACITY = 512
MASKED = 32768.0
M_LEAST = -16384.0
PIECES = 8
CTX_PIECES = [(0, 2), (2, 6), (6, 10), (10, NCH)]
RING = 4
SIDE = 3
LAG = 1

FFN = [dict(fs=96, nk=2, gated=True, act=ACT.Silu, loops=1, alpha=1.0, beta=0.0),
       dict(fs=128, nk=2, gated=True, act=ACT.Silu, loops=2, alpha=1e-9, beta=1.0),
       dict(fs=128, nk=4, gated=False, act=ACT.Gelu, loops=1, alpha=1.0, beta=0.0),
       dict(fs=128, nk=2, gated=True, act=ACT.Silu, loops=1, alpha=0.0, beta=1.0)]


def keys_of(kt):
    return min(P, KEYS - kt * P)


def chunk_of(c):
    return min(CH, KEYS - c * CH)


class Count:

    def __init__(self, handle):
        self.handle, self.n = handle, 0

    def by(self, instruction, step=1):
        instruction.then_inc(self.handle, step)
        self.n += step
        return self.n


def build(nc, A, out):
    ctx = ExitStack()
    with ctx:
        def sb(name, shape, dt=F32):
            return ctx.enter_context(nc.sbuf_tensor(name, shape, dt))

        pe, act, dve, pool, sp = nc.tensor, nc.scalar, nc.vector, nc.gpsimd, nc.sync

        S = ctx.enter_context(nc.psum_tensor("scores", [P, 4, CH], F32))
        MX = ctx.enter_context(nc.psum_tensor("side", [P, SIDE, CH], F32))
        AV = ctx.enter_context(nc.psum_tensor("av", [P, CH], F32))
        MISC = MX[:, 2, :]

        ctxT = sb("ctxT", [P, KEYS])
        xs = sb("xs", [P, NT, D])
        xn = sb("xn", [P, NT, D])
        xnT = sb("xnT", [P, T])
        sq = sb("sq", [P, NT, D])
        stat = sb("stat", [P, 4, NT])
        KA = sb("KA", [P, KEYS], F16)
        KB = sb("KB", [P, KEYS], F16)
        V_all = sb("V_all", [P, KT, HEADS, VC])
        Vst = sb("Vst", [P, KT, HG, VC])
        Qst = sb("Qst", [P, NG, T], F16)
        QPa = sb("QPa", [P, HG, QB], F16)
        QPb = sb("QPb", [P, HG, QB], F16)
        prob = sb("prob", [P, RING, 2 * QB])
        kb32 = sb("kb32", [P, 2, CH])
        hi16 = sb("hi16", [P, 2, CH], F16)
        mpart = sb("mpart", [P, QT, HG, NCH])
        mm = sb("mm", [P, QT, HG])
        Mx = sb("Mx", [P, QT, HG, ROWS])
        oS = sb("oS", [P, QB])
        rden = sb("rden", [P, QT, HG])
        o_tok = sb("o_tok", [P, NT, D])
        cst = sb("cst", [P, 3])
        ident = sb("ident", [P, P])
        upper = sb("upper", [P, P])
        ones = sb("ones", [P, P])
        iota = sb("iota", [P, E])
        aw = [dict(q=sb(f"Wq{i}", [P, NG, P]), k=sb(f"Wk{i}", [P, P]), v=sb(f"Wv{i}", [P, P]),
                   o=sb(f"Wo{i}", [P, P]), b=sb(f"bq{i}", [P, NG]), bk=sb(f"bk{i}", [P, 1]), r=sb(f"bvo{i}", [P, 2, P]))
              for i in range(2)]
        bq = sb("bq", [P, 2, NG])
        lo16 = sb("lo16", [P, 2, CH], F16)
        kparts = nc.dram_tensor("kparts", [2, 2, P, KEYS], F16, kind="Internal").ap()
        Fin = sb("Fin", [P, E, 512])
        Fout = sb("Fout", [P, E, 4, D])
        FinCur = sb("FinCur", [P, 2, 512])
        Wg = sb("Wg", [P, E])
        rbias = sb("rbias", [P, 2, E])
        normw = sb("normw", [P, D])
        b1 = sb("b1", [P, E, 4])
        msum = sb("msum", [P, PIECES])
        mflag = sb("mflag", [P, 2])
        mcount = sb("mcount", [P, 1], I32)
        rowany = sb("rowany", [P, NT])
        vmean = sb("vmean", [P, D])
        bigI = sb("bigI", [P, P], F16)
        b1Cur = sb("b1Cur", [P, EU, 4])
        b2 = sb("b2", [E, D])
        hT = prob[:].rearrange("p r (k c) -> p (r k) c", c=CH).rearrange("p (a b) c -> p a b c", a=2)
        gA = kb32
        yacc = sq
        cwT = kb32[0:E].rearrange("p a c -> p (a c)")
        m8 = sq[:].rearrange("p t d -> p (t d)").bitcast(U8).rearrange("p (a r c) -> p a r c", a=4, r=2)
        m16 = xn[:].rearrange("p t d -> p (t d)").bitcast(F16).rearrange("p (a r c) -> p a r c", a=2, r=2)
        zs = o_tok
        lg = sb("lg", [P, NT, E])
        sel = sb("sel", [P, NT, E])
        top = sb("top", [P, NT, E])
        idx = sb("idx", [P, NT, E], U32)
        idf = sb("idf", [P, NT, E])
        msk = sb("msk", [P, NT, E])
        t1 = sb("t1", [P, NT, E])
        t2 = sb("t2", [P, NT, E])
        cum = sb("cum", [P, NT, E])
        cw = sb("cw", [P, NT, E])
        cwCur = sb("cwCur", [P, NT, EU])
        r1 = sb("r1", [P, 3, NT])

        names = ["seq", "score", "exp", "av", "mxs", "mxr", "qproj", "qsplit", "qstack", "kproj", "kcopy", "ksplit", "kput0", "kput1", "kget", "qready", "ostore",
                 "vstage", "avout", "otr", "dvs", "mtr", "proj", "evac", "stack", "h", "hact", "hready",
                 "y", "yread", "cur", "cwcur", "mload0", "mload1", "mload2", "mload3", "mconv0", "mconv1", "msum"]
        handles = [ctx.enter_context(nc.semaphore("s_" + n)) for n in names]
        sem = {n: Count(h) for n, h in zip(names, handles)}
        cleared = range(min(h.num for h in handles), max(h.num for h in handles) + 1)
        assert len(cleared) == len(handles)
        d_const = Count(ctx.enter_context(nc.semaphore("d_const")))
        d_ctx = [Count(ctx.enter_context(nc.semaphore(f"d_ctx{i}"))) for i in range(len(CTX_PIECES))]
        d_stack = [Count(ctx.enter_context(nc.semaphore(f"d_stack{i}"))) for i in range(4)]
        d_attn = [Count(ctx.enter_context(nc.semaphore(f"d_attn{i}"))) for i in range(4)]
        d_ffn = [Count(ctx.enter_context(nc.semaphore(f"d_ffn{i}"))) for i in range(4)]
        d_out = Count(ctx.enter_context(nc.semaphore("d_out")))

        mask_n, mask_read = [0, 0], {}
        side = {"n": 0, "bank": 0, "read": {}}

        def side_bank():
            side["bank"] = b = side["n"] % SIDE
            side["n"] += 1
            wait(pe, *side["read"].get(b, ("seq", 0)))
            return MX[:, b, :]

        def side_read(name):
            side["read"][side["bank"]] = (name, sem[name].n)

        def barrier():
            nc.all_engine_barrier(sems_to_clear=cleared)
            for c in sem.values():
                c.n = 0
            mask_n[:] = [0, 0]
            mask_read.clear()
            side.update(n=0, read={})

        def wait(eng, name, value=None):
            value = sem[name].n if value is None else value
            if value > 0:
                eng.wait_ge(sem[name].handle, value)

        def after(eng):
            wait(eng, "seq")
            return eng

        def step(instruction):
            sem["seq"].by(instruction)

        def load_attn(l):
            w = aw[l % 2]
            for dst, src in ((w["q"], A[f"Wq{l}"]), (w["k"], A[f"Wk{l}"]), (w["v"], A[f"Wv{l}"]),
                             (w["o"], A[f"Wo{l}"]), (w["b"], A[f"bq{l}"]), (w["bk"], A[f"bk{l}"])):
                d_attn[l].by(sp.dma_start(dst[:], src), 16)
            d_attn[l].by(sp.dma_start(w["r"][:], A[f"bvo{l}"].partition_broadcast(P)), 16)

        def load_ffn(l):
            f = FFN[l]
            nin = f["fs"] * f["nk"] * (2 if f["gated"] else 1)
            d_ffn[l].by(sp.dma_start(Fin[:, :, 0:nin], A[f"Fin{l}"]), 16)
            d_ffn[l].by(sp.dma_start(Fout[0:f["fs"], :, 0:f["nk"], :], A[f"Fout{l}"]), 16)
            d_ffn[l].by(sp.dma_start(Wg[:], A[f"Wg{l}"]), 16)
            if l == 1:
                d_ffn[l].by(sp.dma_start(normw[:], A["normw"].partition_broadcast(P)), 16)
            if l >= 2:
                d_ffn[l].by(sp.dma_start(rbias[:], A[f"rb{l}"].partition_broadcast(P)), 16)
            if l == 3:
                d_ffn[l].by(sp.dma_start(b1[:], A["b1"]), 16)
                d_ffn[l].by(sp.dma_start(b2[:], A["b2"]), 16)

        def loaded(eng, c):
            eng.wait_ge(c.handle, c.n)

        for dst, src in ((xs, A["x"].rearrange("(t p) d -> p t d", p=P)), (cst, A["cst"]),
                         (ident, A["ident"]), (upper, A["upper"]), (ones, A["ones"])):
            d_const.by(sp.dma_start(dst[:], src), 16)
        d_const.by(sp.dma_start(iota[:], A["iota"].partition_broadcast(P)), 16)
        load_attn(0)
        for d, (a, b) in zip(d_ctx, CTX_PIECES):
            part = slice(a * CH, min(b * CH, KEYS))
            d.by(sp.dma_start(ctxT[:, part], A["ctxT"][:, part]), 16)
        gamma, beta, rowc = (cst[:, i:i + 1] for i in range(3))

        for buf in (QPa, QPb):
            pool.memset(buf[:].rearrange("p h q -> p (h q)").bitcast(F32), 0.0)
        pool.memset(V_all[:, :, :, DH:VC], 1.0)
        dve.memset(Mx[:], 0.0)
        dve.memset(KA[:].bitcast(F32), 0.0)
        barrier()

        def broadcast(ap, shape):
            return ap.broadcast_to(shape)

        def norm(dst, src, eps, centre=True, weight=None):
            full = [P, NT, D]
            cur = src
            if centre:
                step(after(dve).tensor_reduce(stat[:, 0, :], src[:], AX.X, ALU.add))
                step(after(dve).tensor_scalar(stat[:, 1, :], stat[:, 0, :], 1.0 / D, None, ALU.mult))
                step(after(dve).tensor_tensor(dst[:], src[:], broadcast(stat[:, 1, :].unsqueeze(2), full), ALU.subtract))
                cur = dst
            step(after(dve).tensor_tensor(sq[:], cur[:], cur[:], ALU.mult))
            step(after(dve).tensor_reduce(stat[:, 2, :], sq[:], AX.X, ALU.add))
            step(after(dve).tensor_scalar(stat[:, 1, :], stat[:, 2, :], 1.0 / D, eps, ALU.mult, ALU.add))
            step(after(act).activation(stat[:, 2, :], stat[:, 1, :], ACT.Sqrt))
            step(after(dve).reciprocal(stat[:, 3, :], stat[:, 2, :]))
            step(after(dve).tensor_tensor(dst[:], cur[:], broadcast(stat[:, 3, :].unsqueeze(2), full), ALU.mult))
            if weight is not None:
                step(after(dve).tensor_tensor(dst[:], dst[:], broadcast(weight[:].unsqueeze(1), full), ALU.mult))

        def transpose_tiles(dst, tile_of):
            for b in range(NQB):
                after(pe)
                for t in range(QT):
                    last = pe.transpose(S[:, b, t * P:(t + 1) * P], tile_of(b * QT + t), ident[:])
                step(last)
            step(after(act).activation(dst[:, 0:CH], S[:, 0, :], ACT.Copy))
            step(after(dve).tensor_copy(dst[:, CH:T], S[:, 1, :]))

        def stack_q(l, i):
            g, qb = i // NQB, i % NQB
            cols = slice(qb * QB, (qb + 1) * QB)
            psum = S[:, i % 4, :]
            wait(pe, "qsplit", i - 3)
            sem["qproj"].by(pe.matmul(psum, aw[l % 2]["q"][:, g, :], xnT[:, cols], start=True, stop=True))
            wait(act, "qproj")
            wait(act, "qstack", i - 1)
            act.activation(hi16[:, i % 2, :], psum, ACT.Identity, bias=bq[:, 1, g:g + 1], scale=gamma)
            sem["qsplit"].by(act.activation(kb32[:, i % 2, :], psum, ACT.Identity, bias=bq[:, 0, g:g + 1], scale=beta))
            wait(dve, "qsplit")
            sem["qstack"].by(dve.tensor_tensor(Qst[:, g, cols], kb32[:, i % 2, :], hi16[:, i % 2, :], ALU.add))

        def project_k(l, c, sub):
            w = chunk_of(c)
            cols = slice(c * CH, c * CH + w)
            slot, used = c % 2, 32 * (c // 2)
            bias = aw[l % 2]["bk"][:]
            bank = side_bank()[:, 0:w]
            sem["kproj"].by(pe.matmul(bank, aw[l % 2]["k"][:], ctxT[:, cols], start=True, stop=True))
            wait(act, "kproj")
            wait(act, f"kput{slot}", used)
            wait(act, "ksplit", c - 1)
            act.activation(hi16[:, slot, 0:w], bank, ACT.Identity, bias=bias)
            sem["kcopy"].by(act.activation(kb32[:, slot, 0:w], bank, ACT.Identity, bias=bias))
            side_read("kcopy")
            wait(sub, "kcopy")
            wait(sub, f"kput{slot}", used)
            sem["ksplit"].by(sub.tensor_tensor(lo16[:, slot, 0:w], kb32[:, slot, 0:w], hi16[:, slot, 0:w], ALU.subtract))
            wait(sp, "kcopy")
            wait(sp, "ksplit")
            for part, buf in enumerate((hi16, lo16)):
                sem[f"kput{slot}"].by(sp.dma_start(kparts[l % 2, part, :, cols], buf[:, slot, 0:w]), 16)

        def project_first_k():
            parts = (KB[:], prob[:].rearrange("p r c -> p (r c)").bitcast(F16)[:, 0:KEYS])
            bias = aw[0]["bk"][:]
            for d, (a, b) in zip(d_ctx, CTX_PIECES):
                loaded(pe, d)
                for c in range(a, b):
                    w = chunk_of(c)
                    cols = slice(c * CH, c * CH + w)
                    bank = side_bank()[:, 0:w]
                    sem["kproj"].by(pe.matmul(bank, aw[0]["k"][:], ctxT[:, cols], start=True, stop=True))
                    wait(act, "kproj")
                    wait(act, "ksplit", c - 1)
                    act.activation(parts[0][:, cols], bank, ACT.Identity, bias=bias)
                    sem["kcopy"].by(act.activation(kb32[:, c % 2, 0:w], bank, ACT.Identity, bias=bias))
                    side_read("kcopy")
                    wait(dve, "kcopy")
                    sem["ksplit"].by(dve.tensor_tensor(parts[1][:, cols], kb32[:, c % 2, 0:w], parts[0][:, cols],
                                                       ALU.subtract))
                wait(sp, "kcopy")
                wait(sp, "ksplit")
                cols = slice(a * CH, min(b * CH, KEYS))
                for part in range(2):
                    sem["kput0"].by(sp.dma_start(kparts[0, part, :, cols], parts[part][:, cols]), 16)
            put_k()

        def put_k():
            wait(sp, "kput0")
            wait(sp, "kput1")

        def get_stack(dst, l, g, count):
            for h in range(HG):
                for block, part in enumerate((0, 0, 1)):
                    row = ROWS * h + DH * block
                    count.by(sp.dma_start(dst[row:row + DH, :], kparts[l % 2, part, bass.ds(g * HG * DH + h * DH, DH), :]), 16)

        def mask_tile(kind, src, n, w):
            i = mask_n[kind]
            mask_n[kind] += 1
            slot = i % 2
            load, conv = f"mload{2 * kind + slot}", f"mconv{kind}"
            wait(sp, conv, i - 1)
            sem[load].by(sp.dma_start(m8[0:n, kind, slot, 0:w], src), 16)
            wait(pool, load)
            wait(pool, *mask_read.get((kind, slot), ("seq", 0)))
            sem[conv].by(pool.tensor_scalar(m16[0:n, kind, slot, 0:w], m8[0:n, kind, slot, 0:w], 1.0, MASKED,
                                            ALU.subtract, ALU.mult))
            wait(pe, conv)
            return m16[0:n, kind, slot, 0:w]

        def read_by(kind, name):
            mask_read[kind, (mask_n[kind] - 1) % 2] = (name, sem[name].n)

        ITEMS = [(qt, c, h) for qt in range(QT) for c in range(NCH) for h in range(HG)]

        def max_product(i, K, QPn, qb, masked, tile):
            qt, c, h = ITEMS[i]
            w = chunk_of(c)
            if masked and h == 0:
                first = (qb * QT + qt) * P
                tile[0] = mask_tile(1, A["mask"][first:first + P, c * CH:c * CH + w], P, w)
            bank = side_bank()[:, 0:w]
            ins = pe.matmul(bank, QPn[:, h, qt * P:(qt + 1) * P], K[:, c * CH:c * CH + w],
                            start=True, stop=not masked)
            if masked:
                ins = pe.matmul(bank, bigI[:], tile[0], start=False, stop=True)
            sem["mxs"].by(ins)
            if masked:
                read_by(1, "mxs")
            wait(dve, "mxs")
            sem["mxr"].by(dve.tensor_reduce(mpart[:, qt, h, c:c + 1], bank, AX.X, ALU.max))
            side_read("mxr")

        def phase(l, probs, ready_q, K, QP, nxt, kprep, pending, store_o, ring, qb, masked):
            softmax = l != 2
            items = []
            if nxt is not None and softmax:
                items = ITEMS
            mtile = [None]
            done = 0
            group_done = {}

            def max_item(i):
                if i == 0:
                    wait(pe, "qready", nxt[3])
                    wait(pe, "kget", nxt[2])
                max_product(i, nxt[0], nxt[1], 1 - qb, masked, mtile)

            mask16 = {}

            def scores(kt, half):
                n = keys_of(kt)
                if masked and half == 0:
                    mask16["tile"] = mask_tile(0, A["maskT"][kt * P:kt * P + n, qb * QB:(qb + 1) * QB], n, QB)
                r = ring["n"]
                ring["n"] += 1
                wait(pe, "exp", r - 1)
                if kt == 0 and half == 0:
                    wait(pe, "qready", ready_q)
                for i in range(2):
                    bank = S[0:n, 2 * (r % 2) + i, :]
                    ins = pe.matmul(bank, K[:, kt * P:kt * P + n], QP[:, 2 * half + i, :], start=True, stop=not masked)
                    if masked:
                        ins = pe.matmul(bank, bigI[0:n, 0:n], mask16["tile"], start=False, stop=True)
                sem["score"].by(ins)
                if masked:
                    read_by(0, "score")
                wait(act, "score")
                wait(act, "av", ring["owner"][r % RING])
                sem["exp"].by(act.activation(
                    probs[0:n, r % RING, :], S[0:n, 2 * (r % 2):2 * (r % 2) + 2, :].rearrange("p a b -> p (a b)"),
                    ACT.Exp if softmax else ACT.Sigmoid, scale=SCALE))
                group_done[2 * kt + half] = (sem["exp"].n, r)

            def attend(kt):
                n = keys_of(kt)
                wait(pe, "exp", group_done[2 * kt + 1][0])
                if kt == 0:
                    wait(pe, "avout")
                    wait(pe, "vstage")
                for h in range(HG):
                    slot = group_done[2 * kt + h // 2][1] % RING
                    ins = pe.matmul(AV[ROWS * h:ROWS * h + VC, :], Vst[0:n, kt, h, :],
                                    probs[0:n, slot, (h % 2) * QB:(h % 2) * QB + QB],
                                    start=kt == 0, stop=kt == KT - 1)
                sem["av"].by(ins)
                for half in range(2):
                    ring["owner"][group_done[2 * kt + half][1] % RING] = sem["av"].n

            def maxima(upto):
                nonlocal done
                while done < len(items) and done * KT * 4 < len(items) * upto:
                    max_item(done)
                    done += 1

            for kt in range(KT + LAG):
                if kt < KT:
                    scores(kt, 0)
                    maxima(4 * kt + 2)
                    scores(kt, 1)
                    maxima(4 * kt + 3)
                    if kt == LAG - 1:
                        for p in pending:
                            p()
                        pending.clear()
                if kt >= LAG:
                    attend(kt - LAG)
                if kt < KT:
                    maxima(4 * kt + 4)
                if kprep and kt >= 3 and (kt - 3) % 3 == 0 and (kt - 3) // 3 < NCH:
                    project_k(l + 1, (kt - 3) // 3, pool)
                if kt == KT - 1 and items:
                    finish_max(nxt[1], masked)

            def output():
                wait(act, "av", av_end)
                wait(act, "otr")
                sem["avout"].by(act.activation(oS[:], AV[:], ACT.Copy))
                wait(pe, "avout")
                bank = side_bank()
                for qt in range(QT):
                    ins = pe.transpose(bank[:, qt * P:(qt + 1) * P], oS[:, qt * P:(qt + 1) * P], ident[:])
                sem["otr"].by(ins)
                wait(dve, "otr")
                o = bank.rearrange("p (q h c) -> p q h c", q=QT, h=HG)
                dst = store_o()
                if softmax:
                    wait(dve, "ostore")
                    if masked:
                        sem["dvs"].by(dve.tensor_scalar(rden[:], o[:, :, :, DH], 1e-30, None, ALU.max))
                        wait(dve, "dvs")
                        sem["dvs"].by(dve.reciprocal(rden[:], rden[:]))
                    else:
                        sem["dvs"].by(dve.reciprocal(rden[:], o[:, :, :, DH]))
                    wait(dve, "dvs")
                    sem["ostore"].by(dve.tensor_tensor(dst, o[:, :, :, 0:DH],
                                                         broadcast(rden[:].unsqueeze(3), [P, QT, HG, DH]), ALU.mult))
                else:
                    sem["ostore"].by(dve.tensor_copy(dst, o[:, :, :, 0:DH]))
                side_read("ostore")

            av_end = sem["av"].n
            pending.append(output)

        def finish_max(QPn, masked):
            wait(dve, "mxr")
            sem["dvs"].by(dve.tensor_reduce(mm[:], mpart[:], AX.X, ALU.max))
            wait(dve, "dvs")
            wait(dve, "mtr")
            if masked:
                sem["dvs"].by(dve.tensor_scalar(mm[:], mm[:], M_LEAST * M_SCALE, None, ALU.max))
                wait(dve, "dvs")
            sem["dvs"].by(dve.tensor_scalar(Mx[:, :, :, M_ROW], mm[:], -1.0 / M_SCALE, None, ALU.mult))
            wait(pe, "dvs")
            bank = side_bank()
            for qt in range(QT):
                ins = pe.transpose(bank[:, qt * P:(qt + 1) * P], Mx[:, qt, :, :].rearrange("p h r -> p (h r)"), ident[:])
            sem["mtr"].by(ins)
            wait(dve, "mtr")
            wait(dve, "mxs")
            for h in range(HG):
                rows = slice(ROWS * h, ROWS * h + ROWS)
                sem["qready"].by(dve.tensor_tensor(QPn[rows, h, :], QPn[rows, h, :], bank[rows, :], ALU.add))
            side_read("qready")

        def fill(QPn, g, qb):
            flat = Qst[:].rearrange("p g t -> p (g t)")
            for h in range(HG):
                rows = slice(ROWS * h, ROWS * h + ROWS)
                sem["qready"].by(dve.tensor_copy(QPn[rows, h, :], flat[rows, bass.ds(g * T + qb * QB, QB)]))

        def stage_v(g):
            src = V_all[:].rearrange("p k h c -> p k (h c)")
            dst = Vst[:].rearrange("p k h c -> p k (h c)")
            w = HG * VC
            full = KT - 1
            pool.tensor_copy(dst[:, 0:full, :], src[:, 0:full, bass.ds(g * w, w)])
            n = keys_of(full)
            sem["vstage"].by(pool.tensor_copy(dst[0:n, full, :], src[0:n, full, bass.ds(g * w, w)]))

        def group(l, g, last, masked=False):
            ring = {"n": 0, "owner": [0] * RING}
            pending = []
            stage_v(g)
            if last and l < 3:
                for eng in (pe, act):
                    loaded(eng, d_attn[l + 1])
            if not last:
                get_stack(KB, l, g + 1, sem["kget"])
            fill(QPb, g, 1)
            q1 = sem["qready"].n

            def store(qb):
                def at():
                    return o_tok[:, qb * QT:(qb + 1) * QT, bass.ds(g * ROWS, ROWS)].rearrange("p q (h c) -> p q h c", h=HG)
                return at

            phase(l, prob, 0, KA, QPa, (KA, QPb, 0, q1), last and l < 3, pending, store(0), ring, 0, masked)
            ready = sem["qready"].n
            nxt = None
            if not last:
                wait(dve, "score")
                fill(QPa, g + 1, 0)
                nxt = (KB, QPa, sem["kget"].n, sem["qready"].n)
            phase(l, prob, ready, KA, QPb, nxt, False, pending, store(1), ring, 1, masked)
            for p in pending:
                p()
            if not last:
                wait(dve, "score")
                wait(dve, "kget")
                step(dve.tensor_copy(KA[:], KB[:]))
            elif l < 3:
                put_k()
            barrier()

        VJ = -(-KT // 4)

        def project_v(l, j):
            bank = side_bank()
            tiles = range(4 * j, min(4 * j + 4, KT))
            for kt in tiles:
                n = keys_of(kt)
                ins = pe.matmul(bank[0:n, (kt % 4) * P:(kt % 4 + 1) * P], ctxT[:, kt * P:kt * P + n],
                                aw[l % 2]["v"][:], start=True, stop=True)
            sem["proj"].by(ins)
            wait(act, "proj")
            for part in ([t for t in tiles if keys_of(t) == P], [t for t in tiles if keys_of(t) < P]):
                if part:
                    a, k, n = part[0], len(part), keys_of(part[0])
                    src = bank[0:n, (a % 4) * P:(a % 4 + k) * P].rearrange("p (k h c) -> p k h c", k=k, h=HEADS)
                    sem["evac"].by(act.activation(V_all[0:n, a:a + k, :, 0:DH], src, ACT.Copy))
            side_read("evac")

        def first_max(l, masked):
            tile = [None]
            every = len(ITEMS) // VJ
            for i in range(len(ITEMS)):
                if i == 0:
                    wait(pe, "qready")
                if not masked and i % every == 0 and i // every < VJ:
                    project_v(l, i // every)
                max_product(i, KA, QPa, 0, masked, tile)
            finish_max(QPa, masked)

        def groups(l, masked):
            with nc.Fori(0, NG - 1) as g:
                group(l, g, False, masked)
            group(l, NG - 1, True, masked)

        def sum_mask():
            n = KEYS * T // P // 2 // PIECES
            assert n * 2 * PIECES * P == KEYS * T and 257 * n < 1 << 24
            flat = A["mask"].rearrange("(p r) k -> p (r k)", p=P)
            both = prob[:].rearrange("p (a r) c -> p a (r c)", a=2).bitcast(U16)
            for i in range(PIECES):
                buf = both[:, i % 2, 0:n]
                wait(sp, "msum", i - 1)
                sem[f"mload{i % 2}"].by(sp.dma_start(buf.bitcast(U8), flat[:, 2 * i * n:2 * (i + 1) * n]), 16)
                wait(act, f"mload{i % 2}")
                sem["msum"].by(act.activation(buf, buf, ACT.Copy, accum_out=msum[:, i:i + 1]))
            wait(dve, "msum")
            sem["dvs"].by(dve.tensor_reduce(mflag[:, 0:1], msum[:], AX.X, ALU.min))
            wait(dve, "dvs")
            sem["dvs"].by(dve.tensor_scalar(mflag[:, 1:2], mflag[:, 0:1], 257.0 * n, None, ALU.is_ge))
            wait(pe, "dvs")
            bank = side_bank()
            sem["msum"].by(pe.matmul(bank[:, 0:1], ones[:], mflag[:, 1:2], start=True, stop=True))
            wait(dve, "msum")
            sem["ostore"].by(dve.tensor_copy(mcount[:], bank[:, 0:1]))
            side_read("ostore")

        def masked_groups():
            step(after(dve).tensor_scalar(bigI[:], ident[:], MASKED, None, ALU.mult))
            fill(QPa, 0, 0)
            for t in range(NT):
                u8 = prob[:].rearrange("p r c -> p (r c)").bitcast(U8)[:, 0:KEYS]
                wait(sp, "msum", t)
                sem["mload0"].by(sp.dma_start(u8, A["mask"][t * P:(t + 1) * P, :]), 16)
                wait(dve, "mload0")
                sem["msum"].by(dve.tensor_reduce(rowany[:, t:t + 1], u8, AX.X, ALU.max))
            barrier()
            first_max(0, True)
            barrier()
            groups(0, True)
            for kt in range(KT):
                n = keys_of(kt)
                last = pe.matmul(MISC[:, 0:HEADS * VC], ones[0:n, :], V_all[0:n, kt, :, :].rearrange("p h c -> p (h c)"),
                                 start=kt == 0, stop=kt == KT - 1)
            step(last)
            mean = MISC[:, 0:HEADS * VC].rearrange("p (h c) -> p h c", h=HEADS)[:, :, 0:DH]
            step(after(dve).tensor_scalar(vmean[:].rearrange("p (h c) -> p h c", h=HEADS), mean, 1.0 / KEYS, None, ALU.mult))
            step(after(dve).tensor_scalar(rowany[:], rowany[:], -1.0, 1.0, ALU.mult, ALU.add))
            for t in range(NT):
                step(after(dve).scalar_tensor_tensor(o_tok[:, t, :], vmean[:], rowany[:, t:t + 1], o_tok[:, t, :],
                                                     ALU.mult, ALU.add))
            barrier()

        def attention(l):
            w = aw[l % 2]
            norm(xn, xs, 1e-5)
            transpose_tiles(xnT, lambda t: xn[:, t, :])
            for eng in (pe, act, dve, pool):
                loaded(eng, d_attn[l])
            for j, factor in enumerate((beta, gamma)):
                step(after(dve).tensor_scalar(bq[:, j, :], w["b"][:], factor, None, ALU.mult))
            wait(act, "seq")
            wait(pe, "seq")
            for i in range(NG * NQB):
                stack_q(l, i)
            if l == 0:
                step(after(dve).tensor_scalar(KA[:], KA[:], rowc, None, ALU.add))
                wait(act, "qstack")
                project_first_k()
                wait(sp, "seq")
                get_stack(KA, 0, 0, d_stack[0])
                wait(dve, "kput0")
                step(dve.memset(KB[:].bitcast(F32), 0.0))
                step(after(dve).tensor_scalar(KB[:], KB[:], rowc, None, ALU.add))
            for eng in (pe, dve):
                loaded(eng, d_stack[l])
            for t in range(QT):
                last = pe.matmul(AV[:, t * P:(t + 1) * P], zeros[:], zeros[:], start=True, stop=True)
            sem["proj"].by(last)
            wait(dve, "qstack")
            fill(QPa, 0, 0)
            if l == 0:
                sum_mask()
            if l != 2:
                first_max(l, False)
            else:
                for j in range(VJ):
                    project_v(l, j)
            barrier()
            if l == 0:
                n = nc.values_load(mcount[0:1, 0:1], min_val=0, max_val=P)
                with nc.If(n == P):
                    groups(l, False)
                with nc.Else():
                    masked_groups()
            else:
                groups(l, False)
            if l != 2:
                step(after(dve).tensor_tensor(o_tok[:], o_tok[:], broadcast(w["r"][:, 0, :].unsqueeze(1), [P, NT, D]), ALU.add))
            transpose_tiles(xnT, lambda t: o_tok[:, t, :])
            for b in range(NQB):
                after(pe)
                for t in range(QT):
                    tt = b * QT + t
                    last = pe.matmul(MX[:, b, t * P:(t + 1) * P], xnT[:, tt * P:(tt + 1) * P], w["o"][:],
                                     start=True, stop=True)
                step(last)
            for b in range(NQB):
                src = MX[:, b, :].rearrange("p (t d) -> p t d", d=D)
                part = xs[:, b * QT:(b + 1) * QT, :]
                step(after(dve).tensor_tensor(part, part, src, ALU.add))
            step(after(dve).tensor_tensor(xs[:], xs[:], broadcast(w["r"][:, 1, :].unsqueeze(1), [P, NT, D]), ALU.add))
            barrier()

        def route(l):
            f = FFN[l]
            full = [P, NT, E]
            L = MISC[:, 0:NT * E].rearrange("p (t e) -> p t e", e=E)
            after(pe)
            for t in range(NT):
                last = pe.matmul(L[:, t, :], xnT[:, t * P:(t + 1) * P], Wg[:], start=True, stop=True)
            step(last)
            if l >= 2:
                step(after(dve).tensor_tensor(lg[:], L, broadcast(rbias[:, 0, :].unsqueeze(1), full), ALU.add))
            else:
                step(after(dve).tensor_copy(lg[:], L))
            by = lg
            if l == 3:
                step(after(dve).tensor_tensor(sel[:], lg[:], broadcast(rbias[:, 1, :].unsqueeze(1), full), ALU.add))
                by = sel
            after(dve)
            for t in range(NT):
                last = dve.max(top[:, t, :], by[:, t, :])
            step(last)
            after(dve)
            for t in range(NT):
                last = dve.max_index(idx[:, t, :], top[:, t, :], by[:, t, :])
            step(last)
            step(after(dve).tensor_copy(idf[:, :, 0:2], idx[:, :, 0:2]))
            io = broadcast(iota[:].unsqueeze(1), full)
            step(after(dve).tensor_tensor(msk[:], io, broadcast(idf[:, :, 0:1], full), ALU.is_equal))
            step(after(dve).tensor_tensor(t1[:], io, broadcast(idf[:, :, 1:2], full), ALU.is_equal))
            step(after(dve).tensor_tensor(msk[:], msk[:], t1[:], ALU.add))
            step(after(dve).tensor_reduce(r1[:, 0, :], lg[:], AX.X, ALU.max))
            step(after(dve).tensor_tensor(t1[:], lg[:], broadcast(r1[:, 0, :].unsqueeze(2), full), ALU.subtract))
            step(after(act).activation(t2[:], t1[:], ACT.Exp))
            step(after(dve).tensor_reduce(r1[:, 1, :], t2[:], AX.X, ALU.add))
            step(after(dve).tensor_tensor(t1[:], t2[:], msk[:], ALU.mult))
            step(after(dve).tensor_reduce(r1[:, 2, :], t1[:], AX.X, ALU.add))
            step(after(dve).tensor_scalar(r1[:, 1, :], r1[:, 1, :], f["alpha"], None, ALU.mult))
            step(after(dve).scalar_tensor_tensor(r1[:, 0, :], r1[:, 2, :], f["beta"], r1[:, 1, :], ALU.mult, ALU.add))
            step(after(dve).reciprocal(r1[:, 1, :], r1[:, 0, :]))
            if l == 0:
                step(after(dve).memset(cum[:, 0, :], 0.0))
                for t in range(NT - 1):
                    step(after(dve).tensor_tensor(cum[:, t + 1, :], cum[:, t, :], msk[:, t, :], ALU.add))
                flat = [a[:].rearrange("p t e -> p (t e)") for a in (msk, cum)]
                after(pe)
                pe.matmul(MISC[:, 0:NT * E], upper[:], flat[0], start=True, stop=False)
                step(pe.matmul(MISC[:, 0:NT * E], ones[:], flat[1], start=False, stop=True))
                step(after(dve).tensor_scalar(t2[:], L, float(CAPACITY), None, ALU.is_lt))
                step(after(dve).tensor_tensor(t1[:], t1[:], t2[:], ALU.mult))
            step(after(dve).tensor_tensor(cw[:], t1[:], broadcast(r1[:, 1, :].unsqueeze(2), full), ALU.mult))

        def experts(l, four):
            f = FFN[l]
            fs, nk, gated = f["fs"], f["nk"], f["gated"]
            nin = fs * nk * (2 if gated else 1)
            flat = Fin[:].rearrange("p e c -> p (e c)")
            w_read = {}

            def stage(k):
                wait(pool, "h", w_read.get(k - 2, 0))
                sem["cur"].by(pool.tensor_copy(FinCur[:, k % 2, 0:nin], flat[:, bass.ds((four * EU + k) * 512, nin)]))
                return sem["cur"].n

            sem["cwcur"].by(dve.tensor_copy(cwCur[:], cw[:, :, bass.ds(four * EU, EU)]))
            if l == 3:
                b1f = b1[:].rearrange("p e c -> p (e c)")
                sem["cwcur"].by(dve.tensor_copy(b1Cur[:].rearrange("p a b -> p (a b)"),
                                                b1f[:, bass.ds(four * EU * 4, EU * 4)]))
            wait(act, "cwcur")
            wait(dve, "cwcur")
            staged = {0: stage(0), 1: stage(1)}
            outf = Fout[:].rearrange("p e k d -> p (e k d)")
            todo = []
            n_act = 0

            def finish(unit, k, b, hbuf, ready):
                bank = MX[:, unit % 2, :]
                wait(pe, "hready", ready)
                wait(pe, "yread", QT * (unit - 1))
                for t in range(QT):
                    for j in range(nk):
                        ins = pe.matmul(bank[:, t * P:(t + 1) * P], hT[0:fs, hbuf, j, t * P:(t + 1) * P],
                                        outf[0:fs, bass.ds(four * EU * 4 * D + (k * 4 + j) * D, D)],
                                        start=j == 0, stop=j == nk - 1)
                sem["y"].by(ins)
                wait(dve, "y")
                for t in range(QT):
                    tt = b * QT + t
                    wait(dve, "yread", sem["yread"].n - QT)
                    sem["yread"].by(dve.scalar_tensor_tensor(yacc[:, tt, :], bank[:, t * P:(t + 1) * P],
                                                             cwCur[:, tt, k:k + 1], yacc[:, tt, :], ALU.mult, ALU.add))

            unit = 0
            for k in range(EU):
                wait(pe, "cur", staged[k])
                for b in range(NQB):
                    hb = unit % 2
                    tok = slice(b * CH, (b + 1) * CH)
                    for j in range(nk):
                        sides = ([j, nk + j] if gated else [j])
                        q = n_act % 2
                        wait(pe, "hready", n_act - 1)
                        for s, col in enumerate(sides):
                            ins = pe.matmul(S[0:fs, 2 * q + s, :], FinCur[:, k % 2, col * fs:(col + 1) * fs], xnT[:, tok],
                                            start=True, stop=True)
                        sem["h"].by(ins)
                        wait(act, "h")
                        wait(act, "y", unit - 1)
                        bias = b1Cur[:, k, j:j + 1] if l == 3 else 0.0
                        if gated:
                            wait(act, "hready", n_act - 1)
                            sem["hact"].by(act.activation(gA[0:fs, q, :], S[0:fs, 2 * q, :], f["act"], bias=bias))
                            wait(dve, "hact")
                            if l == 3:
                                ins = dve.scalar_tensor_tensor(hT[0:fs, hb, j, :], S[0:fs, 2 * q + 1, :],
                                                               b1Cur[:, k, nk + j:nk + j + 1], gA[0:fs, q, :],
                                                               ALU.add, ALU.mult)
                            else:
                                ins = dve.tensor_tensor(hT[0:fs, hb, j, :], S[0:fs, 2 * q + 1, :], gA[0:fs, q, :],
                                                        ALU.mult)
                        else:
                            ins = act.activation(hT[0:fs, hb, j, :], S[0:fs, 2 * q, :], f["act"])
                        sem["hready"].by(ins)
                        n_act += 1
                    if todo:
                        todo.pop(0)()
                    ready = sem["hready"].n

                    def later(unit=unit, k=k, b=b, hb=hb, ready=ready):
                        finish(unit, k, b, hb, ready)
                    todo.append(later)
                    unit += 1
                w_read[k] = sem["h"].n
                if k + 2 < EU:
                    staged[k + 2] = stage(k + 2)
            for x in todo:
                x()
            barrier()

        def ffn(l):
            f = FFN[l]
            if l < 3:
                get_stack(KA, l + 1, 0, d_stack[l + 1])
            for eng in (pe, dve, act, pool):
                loaded(eng, d_ffn[l])
            state = xs
            norm(xn, xs, 1e-5)
            if l == 1:
                state = zs
                step(after(dve).tensor_copy(zs[:], xn[:]))
            for loop in range(f["loops"]):
                if l == 1:
                    norm(xn, zs, 1e-6, centre=False, weight=normw)
                transpose_tiles(xnT, lambda t: xn[:, t, :])
                route(l)
                if l == 3:
                    for b in range(NQB):
                        after(pe)
                        for t in range(QT):
                            last = pe.transpose(S[0:E, b, t * P:(t + 1) * P], cw[:, b * QT + t, :], ident[:])
                        step(last)
                        step(after(dve).tensor_copy(cwT[:, b * CH:(b + 1) * CH], S[0:E, b, :]))
                    for b in range(NQB):
                        after(pe)
                        for t in range(QT):
                            tt = b * QT + t
                            last = pe.matmul(S[:, b, t * P:(t + 1) * P], cwT[:, tt * P:(tt + 1) * P], b2[:],
                                             start=True, stop=True)
                        step(last)
                        step(after(dve).tensor_copy(yacc[:, b * QT:(b + 1) * QT, :],
                                                    S[:, b, :].rearrange("p (t d) -> p t d", d=D)))
                else:
                    step(after(dve).memset(yacc[:], 0.0))
                barrier()
                with nc.Fori(0, E // EU) as four:
                    experts(l, four)
                step(after(dve).tensor_tensor(state[:], state[:], yacc[:], ALU.add))
            if l == 1:
                step(after(dve).tensor_tensor(xs[:], xs[:], zs[:], ALU.add))

        zeros = sb("zeros", [P, P])
        pool.memset(zeros[:], 0.0)
        for eng in (pe, act, dve, pool):
            loaded(eng, d_const)
        barrier()
        for l in range(4):
            load_ffn(l)
            if l < 3:
                load_attn(l + 1)
            attention(l)
            ffn(l)
            barrier()
        d_out.by(sp.dma_start(out.rearrange("(t p) d -> p t d", p=P), xs[:]), 16)
        loaded(sp, d_out)


def _layout(i):
    import numpy as np
    f = np.float32
    a = {}
    a["x"] = np.asarray(i["x"])[0]
    a["mask"] = np.asarray(i["mask_BxSxS2_bf1"])[0].view(np.uint8)
    a["maskT"] = a["mask"].T
    a["ctxT"] = np.asarray(i["ctx_1024"])[0].T

    names = [("L0_xattn_", "Wq bq Wk bk Wv bv Wo bo"), ("L1_xattn_", "W_q b_q W_k b_k W_v b_v W_out b_out"),
             ("L2_xattn_", "Wq - Wk - Wv - Wo -"), ("L3_xattn_", "W_q b_q W_k b_k W_v b_v W_o b_o")]

    def stack(w):
        s = np.zeros((D, NG, HG, 4, DH), f)
        s[:, :, :, 0:3, :] = w.reshape(D, NG, HG, 1, DH)
        return s.reshape(D, NG, P)

    for l, (pre, ns) in enumerate(names):
        wq, bq, wk, bk, wv, bv, wo, bo = (np.zeros(D, f) if n == "-" else np.asarray(i[pre + n]) for n in ns.split())
        a[f"Wq{l}"], a[f"Wk{l}"] = stack(wq.T), wk.T
        a[f"Wv{l}"], a[f"Wo{l}"] = wv.T, wo.T
        a[f"bq{l}"] = stack(np.broadcast_to(bq, (D, D)))[0].T
        a[f"bk{l}"] = bk.reshape(D, 1)
        a[f"bvo{l}"] = np.stack([bv, bo])
    n = {k: np.asarray(v) for k, v in i.items() if "ffn" in k}
    a["Fin0"] = n["L0_ffn_c_fc"].transpose(1, 0, 2)
    a["Fout0"] = n["L0_ffn_c_proj"].reshape(E, 2, 96, D).transpose(2, 0, 1, 3)
    a["Wg0"] = n["L0_ffn_w_gate"]
    a["Fin1"] = np.concatenate([n["L1_ffn_w1"], n["L1_ffn_w3"]], axis=2).transpose(1, 0, 2)
    a["Fout1"] = n["L1_ffn_w2"].reshape(E, 2, P, D).transpose(2, 0, 1, 3)
    a["Wg1"] = n["L1_ffn_router_w"]
    a["normw"] = n["L1_ffn_norm_w"]
    a["Fin2"] = n["L2_ffn_expert_up"].transpose(2, 0, 1)
    a["Fout2"] = n["L2_ffn_expert_down"].transpose(0, 2, 1).reshape(E, 4, P, D).transpose(2, 0, 1, 3)
    a["Wg2"] = n["L2_ffn_router_w"]
    a["rb2"] = np.stack([n["L2_ffn_router_b"], np.zeros(E, f)])
    a["Fin3"] = n["L3_ffn_Wl1"].transpose(1, 0, 2)
    a["Fout3"] = n["L3_ffn_Wl2"].reshape(E, 2, P, D).transpose(2, 0, 1, 3)
    a["Wg3"] = n["L3_ffn_Wr"].T
    a["rb3"] = np.stack([n["L3_ffn_br"], n["L3_ffn_biases_N"]])
    a["b1"] = n["L3_ffn_bl1"].reshape(E, 4, P).transpose(2, 0, 1)
    a["b2"] = n["L3_ffn_bl2"]
    r = np.arange(P) % ROWS
    lo_q = (r >= DH) & (r < 2 * DH)
    a["cst"] = np.stack([np.where(lo_q, -1, 1), lo_q, M_SCALE * (r == M_ROW)], 1).astype(f)
    a["ident"] = np.eye(P, dtype=f)
    a["upper"] = np.triu(np.ones((P, P), f), 1)
    a["ones"] = np.ones((P, P), f)
    a["iota"] = np.arange(E, dtype=f)
    return {k: np.ascontiguousarray(v) for k, v in a.items()}


def kernel(**inputs):
    import concourse.bacc as _bacc
    from concourse import mybir as _mybir
    from concourse.bass_utils import run_bass_kernel_spmd as _run

    nc = _bacc.Bacc("TRN2", target_bir_lowering=False, num_devices=1)
    arrays, args = {}, {}
    for name, a in _layout(inputs).items():
        arrays[f"in_{name}"] = a
        args[name] = nc.dram_tensor(f"in_{name}", a.shape, _mybir.dt.from_np(a.dtype), kind="ExternalInput").ap()
    out = nc.dram_tensor("out_x", (T, D), _mybir.dt.from_np(arrays["in_x"].dtype), kind="ExternalOutput").ap()
    build(nc, args, out)
    r = _run(nc, [arrays], core_ids=[0])
    return r.results[0]["out_x"].reshape(1, T, D)
```

```python
from contextlib import ExitStack

import concourse.bass as bass
from concourse import mybir

ALU = mybir.AluOpType
ACT = mybir.ActivationFunctionType
AX = mybir.AxisListType
F32 = mybir.dt.float32
F16 = mybir.dt.float16
U32 = mybir.dt.uint32
U16 = mybir.dt.uint16
U8 = mybir.dt.uint8
I32 = mybir.dt.int32

P = 128
D = 128
T = 1024
NT = T // P
KEYS = 6404
HEADS, DH = 16, 8
HG = 4
NG = HEADS // HG
ROWS = P // HG
QB = 512
NQB = T // QB
QT = QB // P
KT = -(-KEYS // P)
CH = 512
NCH = -(-KEYS // CH)
VC = DH + 1
M_ROW = 3 * DH
M_SCALE = 64.0
SCALE = float(DH) ** -0.5
E = 8
EU = 4
CAPACITY = 512
MASKED = 32768.0
M_LEAST = -16384.0
FOLD = 4
PIECES = QT * HG
CTX_PIECES = [(0, 2), (2, 6), (6, 10), (10, NCH)]
RING = 4
SIDE = 3
EARLY = 2
V_EARLY, MASK_EARLY = 10, 2
V_NORM, V_LOGITS = 6, 2
V_FIRST = 8
LAG = 1

FFN = [dict(fs=96, nk=2, gated=True, act=ACT.Silu, loops=1, alpha=1.0, beta=0.0),
       dict(fs=128, nk=2, gated=True, act=ACT.Silu, loops=2, alpha=1e-9, beta=1.0),
       dict(fs=128, nk=4, gated=False, act=ACT.Gelu, loops=1, alpha=1.0, beta=0.0),
       dict(fs=128, nk=2, gated=True, act=ACT.Silu, loops=1, alpha=0.0, beta=1.0)]


def keys_of(kt):
    return min(P, KEYS - kt * P)


def chunk_of(c):
    return min(CH, KEYS - c * CH)


class Count:

    def __init__(self, handle):
        self.handle, self.n = handle, 0

    def by(self, instruction, step=1):
        instruction.then_inc(self.handle, step)
        self.n += step
        return self.n


def build(nc, A, out):
    ctx = ExitStack()
    with ctx:
        def sb(name, shape, dt=F32):
            return ctx.enter_context(nc.sbuf_tensor(name, shape, dt))

        pe, act, dve, pool, sp = nc.tensor, nc.scalar, nc.vector, nc.gpsimd, nc.sync

        S = ctx.enter_context(nc.psum_tensor("scores", [P, 4, CH], F32))
        MX = ctx.enter_context(nc.psum_tensor("side", [P, SIDE, CH], F32))
        AV = ctx.enter_context(nc.psum_tensor("av", [P, CH], F32))
        MISC = MX[:, 2, :]

        ctxT = sb("ctxT", [P, KEYS])
        xs = sb("xs", [P, NT, D])
        xn = sb("xn", [P, NT, D])
        xnT = sb("xnT", [P, T])
        sq = sb("sq", [P, NT, D])
        stat = sb("stat", [P, 4, NT])
        KA = sb("KA", [P, KEYS], F16)
        KB = sb("KB", [P, KEYS], F16)
        V_all = sb("V_all", [P, KT, HEADS, VC])
        Vst = sb("Vst", [P, KT, HG, VC])
        Qst = sb("Qst", [P, NG, T], F16)
        QPa = sb("QPa", [P, HG, QB], F16)
        QPb = sb("QPb", [P, HG, QB], F16)
        prob = sb("prob", [P, RING, 2 * QB])
        kb32 = sb("kb32", [P, 2, CH])
        hi16 = sb("hi16", [P, 2, CH], F16)
        mpart = sb("mpart", [P, QT, HG, NCH])
        folds = prob[:].rearrange("p r c -> p (r c)").bitcast(F16).rearrange("p (u j c) -> p u j c", u=2, j=FOLD)
        mm = sb("mm", [P, QT, HG])
        Mx = sb("Mx", [P, QT, HG, ROWS])
        oS = sb("oS", [P, QB])
        rden = sb("rden", [P, QT, HG])
        o_tok = sb("o_tok", [P, NT, D])
        cst = sb("cst", [P, 3])
        ident = sb("ident", [P, P])
        upper = sb("upper", [P, P])
        ones = sb("ones", [P, P])
        iota = sb("iota", [P, E])
        aw = [dict(q=sb(f"Wq{i}", [P, NG, P]), k=sb(f"Wk{i}", [P, P]), v=sb(f"Wv{i}", [P, P]),
                   o=sb(f"Wo{i}", [P, P]), b=sb(f"bq{i}", [P, NG]), bk=sb(f"bk{i}", [P, 1]), r=sb(f"bvo{i}", [P, 2, P]))
              for i in range(2)]
        bq = sb("bq", [P, 2, NG])
        lo16 = sb("lo16", [P, 2, CH], F16)
        kparts = nc.dram_tensor("kparts", [2, 2, P, KEYS], F16, kind="Internal").ap()
        Fin = sb("Fin", [P, E, 512])
        Fout = sb("Fout", [P, E, 4, D])
        FinCur = sb("FinCur", [P, 2, 512])
        Wg = sb("Wg", [P, E])
        rbias = sb("rbias", [P, 2, E])
        normw = sb("normw", [P, D])
        b1 = sb("b1", [P, E, 4])
        msum = sb("msum", [P, PIECES])
        mflag = sb("mflag", [P, 2])
        mcount = sb("mcount", [P, 1], I32)
        rowany = sb("rowany", [P, NT])
        vmean = sb("vmean", [P, D])
        bigI = sb("bigI", [P, P], F16)
        b1Cur = sb("b1Cur", [P, EU, 4])
        b2 = sb("b2", [E, D])
        hT = prob[:].rearrange("p r (k c) -> p (r k) c", c=CH).rearrange("p (a b) c -> p a b c", a=2)
        gA = kb32
        yacc = sq
        cwT = kb32[0:E].rearrange("p a c -> p (a c)")
        m8 = sq[:].rearrange("p t d -> p (t d)").bitcast(U8).rearrange("p (a r c) -> p a r c", a=4, r=2)
        m16 = xn[:].rearrange("p t d -> p (t d)").bitcast(F16).rearrange("p (a r c) -> p a r c", a=2, r=2)
        zs = o_tok
        lg = sb("lg", [P, NT, E])
        sel = sb("sel", [P, NT, E])
        top = sb("top", [P, NT, E])
        idx = sb("idx", [P, NT, E], U32)
        idf = sb("idf", [P, NT, E])
        msk = sb("msk", [P, NT, E])
        t1 = sb("t1", [P, NT, E])
        t2 = sb("t2", [P, NT, E])
        cum = sb("cum", [P, NT, E])
        cw = sb("cw", [P, NT, E])
        cwCur = sb("cwCur", [P, NT, EU])
        r1 = sb("r1", [P, 3, NT])

        names = ["seq", "score", "exp", "av", "mxs", "mxr", "qproj", "qsplit", "qstack", "kproj", "kcopy", "ksplit", "kput0", "kput1", "kget", "qready", "ostore",
                 "vstage", "avout", "otr", "dvs", "mtr", "proj", "evac", "h", "hact", "hready",
                 "y", "yread", "cur", "cwcur", "mload0", "mload1", "mload2", "mload3", "mconv0", "mconv1", "msum",
                 "pair", "copied", "folded"]
        handles = [ctx.enter_context(nc.semaphore("s_" + n)) for n in names]
        sem = {n: Count(h) for n, h in zip(names, handles)}
        cleared = range(min(h.num for h in handles), max(h.num for h in handles) + 1)
        assert len(cleared) == len(handles)
        d_const = Count(ctx.enter_context(nc.semaphore("d_const")))
        d_ctx = [Count(ctx.enter_context(nc.semaphore(f"d_ctx{i}"))) for i in range(len(CTX_PIECES))]
        d_stack = [Count(ctx.enter_context(nc.semaphore(f"d_stack{i}"))) for i in range(4)]
        d_attn = [Count(ctx.enter_context(nc.semaphore(f"d_attn{i}"))) for i in range(4)]
        d_ffn = [Count(ctx.enter_context(nc.semaphore(f"d_ffn{i}"))) for i in range(4)]
        d_out = Count(ctx.enter_context(nc.semaphore("d_out")))

        mask_n, mask_read = [0, 0], {}
        side = {"n": 0, "bank": 0, "read": {}}

        def side_bank(only=None):
            side["bank"] = b = side["n"] % SIDE if only is None else only
            side["n"] += 1
            wait(pe, *side["read"].get(b, ("seq", 0)))
            return MX[:, b, :]

        def side_read(name):
            side["read"][side["bank"]] = (name, sem[name].n)

        def barrier():
            nc.all_engine_barrier(sems_to_clear=cleared)
            for c in sem.values():
                c.n = 0
            mask_n[:] = [0, 0]
            mask_read.clear()
            side.update(n=0, read={})

        def wait(eng, name, value=None):
            value = sem[name].n if value is None else value
            if value > 0:
                eng.wait_ge(sem[name].handle, value)

        def after(eng):
            wait(eng, "seq")
            return eng

        def step(instruction):
            sem["seq"].by(instruction)

        def load_attn(l):
            w = aw[l % 2]
            for dst, src in ((w["q"], A[f"Wq{l}"]), (w["k"], A[f"Wk{l}"]), (w["v"], A[f"Wv{l}"]),
                             (w["o"], A[f"Wo{l}"]), (w["b"], A[f"bq{l}"]), (w["bk"], A[f"bk{l}"])):
                d_attn[l].by(sp.dma_start(dst[:], src), 16)
            d_attn[l].by(sp.dma_start(w["r"][:], A[f"bvo{l}"].partition_broadcast(P)), 16)

        def load_ffn(l):
            f = FFN[l]
            nin = f["fs"] * f["nk"] * (2 if f["gated"] else 1)
            d_ffn[l].by(sp.dma_start(Fin[:, :, 0:nin], A[f"Fin{l}"]), 16)
            d_ffn[l].by(sp.dma_start(Fout[0:f["fs"], :, 0:f["nk"], :], A[f"Fout{l}"]), 16)
            d_ffn[l].by(sp.dma_start(Wg[:], A[f"Wg{l}"]), 16)
            if l == 1:
                d_ffn[l].by(sp.dma_start(normw[:], A["normw"].partition_broadcast(P)), 16)
            if l >= 2:
                d_ffn[l].by(sp.dma_start(rbias[:], A[f"rb{l}"].partition_broadcast(P)), 16)
            if l == 3:
                d_ffn[l].by(sp.dma_start(b1[:], A["b1"]), 16)
                d_ffn[l].by(sp.dma_start(b2[:], A["b2"]), 16)

        def loaded(eng, c):
            eng.wait_ge(c.handle, c.n)

        for dst, src in ((xs, A["x"].rearrange("(t p) d -> p t d", p=P)), (cst, A["cst"]),
                         (ident, A["ident"]), (upper, A["upper"]), (ones, A["ones"])):
            d_const.by(sp.dma_start(dst[:], src), 16)
        d_const.by(sp.dma_start(iota[:], A["iota"].partition_broadcast(P)), 16)
        load_attn(0)
        for d, (a, b) in zip(d_ctx, CTX_PIECES):
            part = slice(a * CH, min(b * CH, KEYS))
            d.by(sp.dma_start(ctxT[:, part], A["ctxT"][:, part]), 16)
        gamma, beta, rowc = (cst[:, i:i + 1] for i in range(3))

        for buf in (QPa, QPb):
            pool.memset(buf[:].rearrange("p h q -> p (h q)").bitcast(F32), 0.0)
        pool.memset(V_all[:, :, :, DH:VC], 1.0)
        dve.memset(Mx[:], 0.0)
        dve.memset(KA[:].bitcast(F32), 0.0)
        barrier()

        def broadcast(ap, shape):
            return ap.broadcast_to(shape)

        def norm(dst, src, eps, centre=True, weight=None):
            full = [P, NT, D]
            cur = src
            if centre:
                step(after(dve).tensor_reduce(stat[:, 0, :], src[:], AX.X, ALU.add))
                step(after(dve).tensor_scalar(stat[:, 1, :], stat[:, 0, :], 1.0 / D, None, ALU.mult))
                step(after(dve).tensor_tensor(dst[:], src[:], broadcast(stat[:, 1, :].unsqueeze(2), full), ALU.subtract))
                cur = dst
            step(after(dve).tensor_tensor(sq[:], cur[:], cur[:], ALU.mult))
            step(after(dve).tensor_reduce(stat[:, 2, :], sq[:], AX.X, ALU.add))
            step(after(dve).tensor_scalar(stat[:, 1, :], stat[:, 2, :], 1.0 / D, eps, ALU.mult, ALU.add))
            step(after(act).activation(stat[:, 2, :], stat[:, 1, :], ACT.Sqrt))
            step(after(dve).reciprocal(stat[:, 3, :], stat[:, 2, :]))
            step(after(dve).tensor_tensor(dst[:], cur[:], broadcast(stat[:, 3, :].unsqueeze(2), full), ALU.mult))
            if weight is not None:
                step(after(dve).tensor_tensor(dst[:], dst[:], broadcast(weight[:].unsqueeze(1), full), ALU.mult))

        def transpose_tiles(dst, tile_of):
            for b in range(NQB):
                after(pe)
                for t in range(QT):
                    last = pe.transpose(S[:, b, t * P:(t + 1) * P], tile_of(b * QT + t), ident[:])
                step(last)
            step(after(act).activation(dst[:, 0:CH], S[:, 0, :], ACT.Copy))
            step(after(dve).tensor_copy(dst[:, CH:T], S[:, 1, :]))

        def stack_q(l, i):
            g, qb = i // NQB, i % NQB
            cols = slice(qb * QB, (qb + 1) * QB)
            psum = side_bank()
            sem["qproj"].by(pe.matmul(psum, aw[l % 2]["q"][:, g, :], xnT[:, cols], start=True, stop=True))
            wait(act, "qproj")
            wait(act, "qstack", i - 1)
            act.activation(hi16[:, i % 2, :], psum, ACT.Identity, bias=bq[:, 1, g:g + 1], scale=gamma)
            sem["qsplit"].by(act.activation(kb32[:, i % 2, :], psum, ACT.Identity, bias=bq[:, 0, g:g + 1], scale=beta))
            side_read("qsplit")
            wait(dve, "qsplit")
            sem["qstack"].by(dve.tensor_tensor(Qst[:, g, cols], kb32[:, i % 2, :], hi16[:, i % 2, :], ALU.add))

        def project_k(l, c, sub, only, idle):
            w = chunk_of(c)
            cols = slice(c * CH, c * CH + w)
            slot, used = c % 2, 32 * (c // 2)
            bias = aw[l % 2]["bk"][:]
            bank = side_bank(only)[:, 0:w]
            sem["kproj"].by(pe.matmul(bank, aw[l % 2]["k"][:], ctxT[:, cols], start=True, stop=True))
            eng = dve if idle else act
            wait(eng, "kproj")
            wait(eng, f"kput{slot}", used)
            wait(eng, "ksplit", c - 1)
            for buf in (hi16, kb32):
                if idle:
                    ins = dve.tensor_scalar(buf[:, slot, 0:w], bank, bias, None, ALU.add)
                else:
                    ins = act.activation(buf[:, slot, 0:w], bank, ACT.Identity, bias=bias)
            sem["kcopy"].by(ins)
            side_read("kcopy")
            wait(sub, "kcopy")
            wait(sub, f"kput{slot}", used)
            sem["ksplit"].by(sub.tensor_tensor(lo16[:, slot, 0:w], kb32[:, slot, 0:w], hi16[:, slot, 0:w], ALU.subtract))
            wait(sp, "kcopy")
            wait(sp, "ksplit")
            for part, buf in enumerate((hi16, lo16)):
                sem[f"kput{slot}"].by(sp.dma_start(kparts[l % 2, part, :, cols], buf[:, slot, 0:w]), 16)

        def project_first_k():
            parts = (KB[:], prob[:].rearrange("p r c -> p (r c)").bitcast(F16)[:, 0:KEYS])
            bias = aw[0]["bk"][:]
            for d, (a, b) in zip(d_ctx, CTX_PIECES):
                loaded(pe, d)
                for c in range(a, b):
                    w = chunk_of(c)
                    cols = slice(c * CH, c * CH + w)
                    bank = side_bank()[:, 0:w]
                    sem["kproj"].by(pe.matmul(bank, aw[0]["k"][:], ctxT[:, cols], start=True, stop=True))
                    wait(act, "kproj")
                    wait(act, "ksplit", c - 1)
                    act.activation(parts[0][:, cols], bank, ACT.Identity, bias=bias)
                    sem["kcopy"].by(act.activation(kb32[:, c % 2, 0:w], bank, ACT.Identity, bias=bias))
                    side_read("kcopy")
                    wait(dve, "kcopy")
                    sem["ksplit"].by(dve.tensor_tensor(parts[1][:, cols], kb32[:, c % 2, 0:w], parts[0][:, cols],
                                                       ALU.subtract))
                wait(sp, "kcopy")
                wait(sp, "ksplit")
                cols = slice(a * CH, min(b * CH, KEYS))
                for part in range(2):
                    sem["kput0"].by(sp.dma_start(kparts[0, part, :, cols], parts[part][:, cols]), 16)
            put_k()

        def put_k():
            wait(sp, "kput0")
            wait(sp, "kput1")

        def get_stack(dst, l, g, count):
            for h in range(HG):
                for block, part in enumerate((0, 0, 1)):
                    row = ROWS * h + DH * block
                    count.by(sp.dma_start(dst[row:row + DH, :], kparts[l % 2, part, bass.ds(g * HG * DH + h * DH, DH), :]), 16)

        def mask_tile(kind, src, n, w):
            i = mask_n[kind]
            mask_n[kind] += 1
            slot = i % 2
            load, conv = f"mload{2 * kind + slot}", f"mconv{kind}"
            wait(sp, conv, i - 1)
            sem[load].by(sp.dma_start(m8[0:n, kind, slot, 0:w], src), 16)
            wait(pool, load)
            wait(pool, *mask_read.get((kind, slot), ("seq", 0)))
            sem[conv].by(pool.tensor_scalar(m16[0:n, kind, slot, 0:w], m8[0:n, kind, slot, 0:w], 1.0, MASKED,
                                            ALU.subtract, ALU.mult))
            wait(pe, conv)
            return m16[0:n, kind, slot, 0:w]

        def read_by(kind, name):
            mask_read[kind, (mask_n[kind] - 1) % 2] = (name, sem[name].n)

        ITEMS = [(qt, c, h) for qt in range(QT) for c in range(NCH) for h in range(HG)]

        def max_product(i, K, QPn, qb, masked, tile):
            qt, c, h = ITEMS[i]
            w = chunk_of(c)
            if masked and h == 0:
                first = (qb * QT + qt) * P
                tile[0] = mask_tile(1, A["mask"][first:first + P, c * CH:c * CH + w], P, w)
            bank = side_bank()[:, 0:w]
            ins = pe.matmul(bank, QPn[:, h, qt * P:(qt + 1) * P], K[:, c * CH:c * CH + w],
                            start=True, stop=not masked)
            if masked:
                ins = pe.matmul(bank, bigI[:], tile[0], start=False, stop=True)
            sem["mxs"].by(ins)
            if masked:
                read_by(1, "mxs")
            wait(dve, "mxs")
            sem["mxr"].by(dve.tensor_reduce(mpart[:, qt, h, c:c + 1], bank, AX.X, ALU.max))
            side_read("mxr")

        def phase(l, probs, ready_q, K, QP, nxt, kprep, pending, store_o, ring, qb, masked):
            softmax = l != 2
            pairs, only = (2, None) if softmax and nxt is not None else (3, SIDE - 1)
            drained = sem["exp"].n if ring["pairs"] != pairs else 0
            ring["pairs"], ring["only"] = pairs, only
            items = []
            if nxt is not None and softmax:
                items = ITEMS
            mtile = [None]
            done = 0
            group_done = {}

            def max_item(i):
                if i == 0:
                    wait(pe, "qready", nxt[3])
                    wait(pe, "kget", nxt[2])
                max_product(i, nxt[0], nxt[1], 1 - qb, masked, mtile)

            mask16 = {}

            def scores(kt, half):
                n = keys_of(kt)
                if masked and half == 0:
                    mask16["tile"] = mask_tile(0, A["maskT"][kt * P:kt * P + n, qb * QB:(qb + 1) * QB], n, QB)
                r = ring["n"]
                ring["n"] += 1
                wait(pe, "exp", max(r - pairs + 1, drained))
                if pairs == 3 and r % pairs == 2:
                    for b in range(2):
                        wait(pe, *side["read"].pop(b, ("seq", 0)))
                pair = S[:, 2 * (r % pairs):2 * (r % pairs) + 2, :] if r % pairs < 2 else MX[:, 0:2, :]
                if kt == 0 and half == 0:
                    wait(pe, "qready", ready_q)
                for i in range(2):
                    bank = pair[0:n, i, :]
                    ins = pe.matmul(bank, K[:, kt * P:kt * P + n], QP[:, 2 * half + i, :], start=True, stop=not masked)
                    if masked:
                        ins = pe.matmul(bank, bigI[0:n, 0:n], mask16["tile"], start=False, stop=True)
                sem["score"].by(ins)
                if masked:
                    read_by(0, "score")
                wait(act, "score")
                wait(act, "av", ring["owner"][r % RING])
                sem["exp"].by(act.activation(
                    probs[0:n, r % RING, :], pair[0:n].rearrange("p a b -> p (a b)"),
                    ACT.Exp if softmax else ACT.Sigmoid, scale=SCALE))
                group_done[2 * kt + half] = (sem["exp"].n, r)

            def attend(kt):
                n = keys_of(kt)
                wait(pe, "exp", group_done[2 * kt + 1][0])
                if kt == 0:
                    wait(pe, "avout")
                wait(pe, "vstage", 1 if kt < V_FIRST else 2)
                for h in range(HG):
                    slot = group_done[2 * kt + h // 2][1] % RING
                    ins = pe.matmul(AV[ROWS * h:ROWS * h + VC, :], Vst[0:n, kt, h, :],
                                    probs[0:n, slot, (h % 2) * QB:(h % 2) * QB + QB],
                                    start=kt == 0, stop=kt == KT - 1)
                sem["av"].by(ins)
                for half in range(2):
                    ring["owner"][group_done[2 * kt + half][1] % RING] = sem["av"].n

            def maxima(upto):
                nonlocal done
                while done < len(items) and done * (KT - EARLY) * 4 < len(items) * upto:
                    max_item(done)
                    done += 1

            for kt in range(KT + LAG):
                if kt < KT:
                    scores(kt, 0)
                    maxima(4 * kt + 2)
                    scores(kt, 1)
                    maxima(4 * kt + 3)
                    if kt in (LAG - 1, LAG) and pending:
                        pending.pop(0)()
                if kt >= LAG:
                    attend(kt - LAG)
                if kt < KT:
                    maxima(4 * kt + 4)
                if kprep and kt >= 3 and (kt - 3) % 3 == 0 and (kt - 3) // 3 < NCH:
                    project_k(l + 1, (kt - 3) // 3, pool, only, not softmax)
                if kt == KT - EARLY and items:
                    finish_max(nxt[1], masked)

            def drain_av():
                wait(act, "av", av_end)
                wait(act, "otr")
                sem["avout"].by(act.activation(oS[:], AV[:], ACT.Copy))

            def output():
                wait(pe, "avout")
                bank = side_bank(ring["only"])
                for qt in range(QT):
                    ins = pe.transpose(bank[:, qt * P:(qt + 1) * P], oS[:, qt * P:(qt + 1) * P], ident[:])
                sem["otr"].by(ins)
                wait(dve, "otr")
                o = bank.rearrange("p (q h c) -> p q h c", q=QT, h=HG)
                dst = store_o()
                if softmax:
                    wait(dve, "ostore")
                    if masked:
                        sem["dvs"].by(dve.tensor_scalar(rden[:], o[:, :, :, DH], 1e-30, None, ALU.max))
                        wait(dve, "dvs")
                        sem["dvs"].by(dve.reciprocal(rden[:], rden[:]))
                    else:
                        sem["dvs"].by(dve.reciprocal(rden[:], o[:, :, :, DH]))
                    wait(dve, "dvs")
                    sem["ostore"].by(dve.tensor_tensor(dst, o[:, :, :, 0:DH],
                                                         broadcast(rden[:].unsqueeze(3), [P, QT, HG, DH]), ALU.mult))
                else:
                    sem["ostore"].by(dve.tensor_copy(dst, o[:, :, :, 0:DH]))
                side_read("ostore")

            av_end = sem["av"].n
            pending.extend([drain_av, output])

        def finish_max(QPn, masked):
            wait(dve, "mxr")
            sem["dvs"].by(dve.tensor_reduce(mm[:], mpart[:], AX.X, ALU.max))
            wait(dve, "dvs")
            wait(dve, "mtr")
            if masked:
                sem["dvs"].by(dve.tensor_scalar(mm[:], mm[:], M_LEAST * M_SCALE, None, ALU.max))
                wait(dve, "dvs")
            sem["dvs"].by(dve.tensor_scalar(Mx[:, :, :, M_ROW], mm[:], -1.0 / M_SCALE, None, ALU.mult))
            wait(pe, "dvs")
            bank = side_bank()
            for qt in range(QT):
                ins = pe.transpose(bank[:, qt * P:(qt + 1) * P], Mx[:, qt, :, :].rearrange("p h r -> p (h r)"), ident[:])
            sem["mtr"].by(ins)
            wait(dve, "mtr")
            wait(dve, "mxs")
            for h in range(HG):
                rows = slice(ROWS * h, ROWS * h + ROWS)
                sem["qready"].by(dve.tensor_tensor(QPn[rows, h, :], QPn[rows, h, :], bank[rows, :], ALU.add))
            side_read("qready")

        def fill(QPn, g, qb):
            flat = Qst[:].rearrange("p g t -> p (g t)")
            for h in range(HG):
                rows = slice(ROWS * h, ROWS * h + ROWS)
                sem["qready"].by(dve.tensor_copy(QPn[rows, h, :], flat[rows, bass.ds(g * T + qb * QB, QB)]))

        def stage_v(g):
            src = V_all[:].rearrange("p k h c -> p k (h c)")
            dst = Vst[:].rearrange("p k h c -> p k (h c)")
            w = HG * VC
            full = KT - 1
            for a, b in ((0, V_FIRST), (V_FIRST, full)):
                ins = pool.tensor_copy(dst[:, a:b, :], src[:, a:b, bass.ds(g * w, w)])
                if a == 0:
                    sem["vstage"].by(ins)
            n = keys_of(full)
            sem["vstage"].by(pool.tensor_copy(dst[0:n, full, :], src[0:n, full, bass.ds(g * w, w)]))

        def group(l, g, last, masked=False):
            ring = {"n": 0, "owner": [0] * RING, "pairs": 2}
            pending = []
            stage_v(g)
            if last and l < 3:
                for eng in (pe, act, dve):
                    loaded(eng, d_attn[l + 1])
            if not last:
                get_stack(KB, l, g + 1, sem["kget"])
            fill(QPb, g, 1)
            q1 = sem["qready"].n

            def store(qb):
                def at():
                    return o_tok[:, qb * QT:(qb + 1) * QT, bass.ds(g * ROWS, ROWS)].rearrange("p q (h c) -> p q h c", h=HG)
                return at

            phase(l, prob, 0, KA, QPa, (KA, QPb, 0, q1), last and l < 3, pending, store(0), ring, 0, masked)
            ready = sem["qready"].n
            nxt = None
            if not last:
                wait(dve, "score")
                fill(QPa, g + 1, 0)
                nxt = (KB, QPa, sem["kget"].n, sem["qready"].n)
            phase(l, prob, ready, KA, QPb, nxt, False, pending, store(1), ring, 1, masked)
            if not last:
                wait(dve, "score")
                wait(dve, "kget")
                step(dve.tensor_copy(KA[:], KB[:]))
            for p in pending:
                p()
            if last and l < 3:
                put_k()
            barrier()

        VJ = -(-KT // 4)

        def project_v(l, j, only=None):
            bank = side_bank(only)
            tiles = range(4 * j, min(4 * j + 4, KT))
            for kt in tiles:
                n = keys_of(kt)
                ins = pe.matmul(bank[0:n, (kt % 4) * P:(kt % 4 + 1) * P], ctxT[:, kt * P:kt * P + n],
                                aw[l % 2]["v"][:], start=True, stop=True)
            sem["proj"].by(ins)
            wait(act, "proj")
            for part in ([t for t in tiles if keys_of(t) == P], [t for t in tiles if keys_of(t) < P]):
                if part:
                    a, k, n = part[0], len(part), keys_of(part[0])
                    src = bank[0:n, (a % 4) * P:(a % 4 + k) * P].rearrange("p (k h c) -> p k h c", k=k, h=HEADS)
                    sem["evac"].by(act.activation(V_all[0:n, a:a + k, :, 0:DH], src, ACT.Copy))
            side_read("evac")

        def first_max(masked):
            tile = [None]
            wait(pe, "qready")
            for i in range(len(ITEMS)):
                max_product(i, KA, QPa, 0, masked, tile)
            finish_max(QPa, masked)

        def open_layer(l, extra):
            wait(pe, "qready")
            steps = []

            def fold(step_, *operands):
                wait(dve, "folded")
                sem["folded"].by(step_(*operands))

            def folds_of(u, qt, h, copied):
                buf = folds[:, u % 2]

                def halves(x, width):
                    return lambda: fold(dve.tensor_tensor, x[:, 0:width], x[:, 0:width], x[:, width:2 * width], ALU.max)
                flat = buf.rearrange("p j c -> p (j c)")
                w = FOLD * CH

                def first():
                    wait(dve, "copied", copied)
                    halves(flat, w)()
                todo = [first]
                while w > CH // 2:
                    w //= 2
                    todo.append(halves(flat, w))
                todo.append(lambda: fold(dve.tensor_reduce, mpart[:, qt, h, 0:2 * FOLD],
                                         flat[:, 0:w].rearrange("p (a b) -> p a b", a=2 * FOLD), AX.X, ALU.max))
                return todo

            folded = []
            for u, (qt, h) in enumerate((qt, h) for qt in range(QT) for h in range(HG)):
                if l == 0 and V_EARLY <= u + V_EARLY < VJ:
                    project_v(l, u + V_EARLY)
                if 0 < u < NG * NQB:
                    stack_q(l, u)
                for x in extra[u]:
                    x()
                for j in range(FOLD):
                    n = sem["pair"].n
                    wait(pe, "copied", n - 1)
                    pair = S[:, 2 * (n % 2):2 * (n % 2) + 2, :]
                    for i in range(2):
                        c = 2 * j + i
                        ins = pe.matmul(pair[:, i, :], QPa[:, h, qt * P:(qt + 1) * P], KA[:, c * CH:(c + 1) * CH],
                                        start=True, stop=True)
                    sem["pair"].by(ins)
                    wait(act, "pair")
                    if u >= 2 and j == 0:
                        wait(act, "folded", folded[u - 2])
                    sem["copied"].by(act.activation(folds[:, u % 2, j, :], pair.rearrange("p a b -> p (a b)"), ACT.Copy,
                                                    scale=1.0 / M_SCALE))
                    if steps:
                        steps.pop(0)()
                    max_product((qt * NCH + 2 * FOLD + j) * HG + h, KA, QPa, 0, False, None)
                for c in range(3 * FOLD, NCH):
                    max_product((qt * NCH + c) * HG + h, KA, QPa, 0, False, None)
                for x in steps:
                    x()
                if u:
                    folded.append(sem["folded"].n)
                steps = folds_of(u, qt, h, sem["copied"].n)
            for x in steps:
                x()
            wait(dve, "folded")
            part = mpart[:, :, :, 0:2 * FOLD]
            sem["mxr"].by(dve.tensor_scalar(part, part, M_SCALE, None, ALU.mult))
            finish_max(QPa, False)

        def groups(l, masked):
            with nc.Fori(0, NG - 1) as g:
                group(l, g, False, masked)
            group(l, NG - 1, True, masked)

        MASK_N = KEYS * T // P // 2 // PIECES
        assert MASK_N * 2 * PIECES * P == KEYS * T and 257 * MASK_N < 1 << 24

        def sum_mask(i):
            flat = A["mask"].rearrange("(p r) k -> p (r k)", p=P)
            both = Vst[:].rearrange("p k h c -> p (k h c)").bitcast(U16)
            first = (i % 2) * (MASK_N + MASK_N % 2)
            buf = both[:, first:first + MASK_N]
            wait(sp, "msum", i - 1)
            sem[f"mload{i % 2}"].by(sp.dma_start(buf.bitcast(U8), flat[:, 2 * i * MASK_N:2 * (i + 1) * MASK_N]), 16)
            wait(act, f"mload{i % 2}")
            sem["msum"].by(act.activation(buf, buf, ACT.Copy, accum_out=msum[:, i:i + 1]))

        def count_mask():
            wait(dve, "msum")
            sem["dvs"].by(dve.tensor_reduce(mflag[:, 0:1], msum[:], AX.X, ALU.min))
            wait(dve, "dvs")
            sem["dvs"].by(dve.tensor_scalar(mflag[:, 1:2], mflag[:, 0:1], 257.0 * MASK_N, None, ALU.is_ge))
            wait(pe, "dvs")
            bank = side_bank()
            sem["msum"].by(pe.matmul(bank[:, 0:1], ones[:], mflag[:, 1:2], start=True, stop=True))
            wait(dve, "msum")
            sem["ostore"].by(dve.tensor_copy(mcount[:], bank[:, 0:1]))
            side_read("ostore")

        def masked_groups():
            step(after(dve).tensor_scalar(bigI[:], ident[:], MASKED, None, ALU.mult))
            fill(QPa, 0, 0)
            for t in range(NT):
                u8 = prob[:].rearrange("p r c -> p (r c)").bitcast(U8)[:, 0:KEYS]
                wait(sp, "msum", t)
                sem["mload0"].by(sp.dma_start(u8, A["mask"][t * P:(t + 1) * P, :]), 16)
                wait(dve, "mload0")
                sem["msum"].by(dve.tensor_reduce(rowany[:, t:t + 1], u8, AX.X, ALU.max))
            barrier()
            first_max(True)
            barrier()
            groups(0, True)
            for kt in range(KT):
                n = keys_of(kt)
                last = pe.matmul(MISC[:, 0:HEADS * VC], ones[0:n, :], V_all[0:n, kt, :, :].rearrange("p h c -> p (h c)"),
                                 start=kt == 0, stop=kt == KT - 1)
            step(last)
            mean = MISC[:, 0:HEADS * VC].rearrange("p (h c) -> p h c", h=HEADS)[:, :, 0:DH]
            step(after(dve).tensor_scalar(vmean[:].rearrange("p (h c) -> p h c", h=HEADS), mean, 1.0 / KEYS, None, ALU.mult))
            step(after(dve).tensor_scalar(rowany[:], rowany[:], -1.0, 1.0, ALU.mult, ALU.add))
            for t in range(NT):
                step(after(dve).scalar_tensor_tensor(o_tok[:, t, :], vmean[:], rowany[:, t:t + 1], o_tok[:, t, :],
                                                     ALU.mult, ALU.add))
            barrier()

        def attention(l):
            w = aw[l % 2]
            norm(xn, xs, 1e-5)
            for eng in (pe, act, dve, pool):
                loaded(eng, d_attn[l])
            for j, factor in enumerate((beta, gamma)):
                step(after(dve).tensor_scalar(bq[:, j, :], w["b"][:], factor, None, ALU.mult))
            transpose_tiles(xnT, lambda t: xn[:, t, :])
            wait(act, "seq")
            wait(pe, "seq")
            stack_q(l, 0)
            if l == 0:
                step(after(dve).tensor_scalar(KA[:], KA[:], rowc, None, ALU.add))
                wait(act, "qstack")
                project_first_k()
                wait(sp, "seq")
                get_stack(KA, 0, 0, d_stack[0])
                wait(dve, "kput0")
                step(dve.memset(KB[:].bitcast(F32), 0.0))
                step(after(dve).tensor_scalar(KB[:], KB[:], rowc, None, ALU.add))
            if l == 0:
                for j in range(V_EARLY):
                    project_v(0, j)
                for i in range(MASK_EARLY):
                    sum_mask(i)
            for eng in (pe, dve):
                loaded(eng, d_stack[l])
            if l == 0:
                for t in range(QT):
                    last = pe.matmul(AV[:, t * P:(t + 1) * P], zeros[:], zeros[:], start=True, stop=True)
                sem["proj"].by(last)
            wait(dve, "qstack")
            fill(QPa, 0, 0)
            if l != 2:
                open_layer(l, [[lambda i=i: sum_mask(i)] if l == 0 and i >= MASK_EARLY else [] for i in range(PIECES)])
            else:
                for i in range(1, NG * NQB):
                    stack_q(l, i)
            if l == 0:
                count_mask()
            barrier()
            if l == 0:
                n = nc.values_load(mcount[0:1, 0:1], min_val=0, max_val=P)
                with nc.If(n == P):
                    groups(l, False)
                with nc.Else():
                    masked_groups()
            else:
                groups(l, False)
            if l != 2:
                step(after(dve).tensor_tensor(o_tok[:], o_tok[:], broadcast(w["r"][:, 0, :].unsqueeze(1), [P, NT, D]), ALU.add))
            transpose_tiles(xnT, lambda t: o_tok[:, t, :])
            for b in range(NQB):
                after(pe)
                for t in range(QT):
                    tt = b * QT + t
                    last = pe.matmul(MX[:, b, t * P:(t + 1) * P], xnT[:, tt * P:(tt + 1) * P], w["o"][:],
                                     start=True, stop=True)
                step(last)
            for b in range(NQB):
                src = MX[:, b, :].rearrange("p (t d) -> p t d", d=D)
                part = xs[:, b * QT:(b + 1) * QT, :]
                step(after(dve).tensor_tensor(part, part, src, ALU.add))
            step(after(dve).tensor_tensor(xs[:], xs[:], broadcast(w["r"][:, 1, :].unsqueeze(1), [P, NT, D]), ALU.add))
            barrier()

        def route(l, beside):
            f = FFN[l]
            full = [P, NT, E]
            L = MISC[:, 0:NT * E].rearrange("p (t e) -> p t e", e=E)
            after(pe)
            for t in range(NT):
                last = pe.matmul(L[:, t, :], xnT[:, t * P:(t + 1) * P], Wg[:], start=True, stop=True)
            step(last)
            logits = sem["seq"].n
            for x in beside[:V_LOGITS]:
                x()
            wait(dve, "seq", logits)
            if l >= 2:
                step(after(dve).tensor_tensor(lg[:], L, broadcast(rbias[:, 0, :].unsqueeze(1), full), ALU.add))
            else:
                step(after(dve).tensor_copy(lg[:], L))
            by = lg
            if l == 3:
                step(after(dve).tensor_tensor(sel[:], lg[:], broadcast(rbias[:, 1, :].unsqueeze(1), full), ALU.add))
                by = sel
            after(dve)
            for t in range(NT):
                last = dve.max(top[:, t, :], by[:, t, :])
            step(last)
            after(dve)
            for t in range(NT):
                last = dve.max_index(idx[:, t, :], top[:, t, :], by[:, t, :])
            step(last)
            step(after(dve).tensor_copy(idf[:, :, 0:2], idx[:, :, 0:2]))
            io = broadcast(iota[:].unsqueeze(1), full)
            step(after(dve).tensor_tensor(msk[:], io, broadcast(idf[:, :, 0:1], full), ALU.is_equal))
            step(after(dve).tensor_tensor(t1[:], io, broadcast(idf[:, :, 1:2], full), ALU.is_equal))
            step(after(dve).tensor_tensor(msk[:], msk[:], t1[:], ALU.add))
            step(after(dve).tensor_reduce(r1[:, 0, :], lg[:], AX.X, ALU.max))
            step(after(dve).tensor_tensor(t1[:], lg[:], broadcast(r1[:, 0, :].unsqueeze(2), full), ALU.subtract))
            step(after(act).activation(t2[:], t1[:], ACT.Exp))
            for x in beside[V_LOGITS:]:
                x()
            step(after(dve).tensor_reduce(r1[:, 1, :], t2[:], AX.X, ALU.add))
            step(after(dve).tensor_tensor(t1[:], t2[:], msk[:], ALU.mult))
            step(after(dve).tensor_reduce(r1[:, 2, :], t1[:], AX.X, ALU.add))
            step(after(dve).tensor_scalar(r1[:, 1, :], r1[:, 1, :], f["alpha"], None, ALU.mult))
            step(after(dve).scalar_tensor_tensor(r1[:, 0, :], r1[:, 2, :], f["beta"], r1[:, 1, :], ALU.mult, ALU.add))
            step(after(dve).reciprocal(r1[:, 1, :], r1[:, 0, :]))
            if l == 0:
                step(after(dve).memset(cum[:, 0, :], 0.0))
                for t in range(NT - 1):
                    step(after(dve).tensor_tensor(cum[:, t + 1, :], cum[:, t, :], msk[:, t, :], ALU.add))
                flat = [a[:].rearrange("p t e -> p (t e)") for a in (msk, cum)]
                after(pe)
                pe.matmul(MISC[:, 0:NT * E], upper[:], flat[0], start=True, stop=False)
                step(pe.matmul(MISC[:, 0:NT * E], ones[:], flat[1], start=False, stop=True))
                step(after(dve).tensor_scalar(t2[:], L, float(CAPACITY), None, ALU.is_lt))
                step(after(dve).tensor_tensor(t1[:], t1[:], t2[:], ALU.mult))
            step(after(dve).tensor_tensor(cw[:], t1[:], broadcast(r1[:, 1, :].unsqueeze(2), full), ALU.mult))

        def experts(l, four):
            f = FFN[l]
            fs, nk, gated = f["fs"], f["nk"], f["gated"]
            nin = fs * nk * (2 if gated else 1)
            flat = Fin[:].rearrange("p e c -> p (e c)")
            w_read = {}

            def stage(k):
                wait(pool, "h", w_read.get(k - 2, 0))
                name, eng = ("cur", pool) if k else ("cwcur", dve)
                sem[name].by(eng.tensor_copy(FinCur[:, k % 2, 0:nin], flat[:, bass.ds((four * EU + k) * 512, nin)]))
                return name, sem[name].n

            staged = {0: stage(0), 1: stage(1)}
            sem["cwcur"].by(dve.tensor_copy(cwCur[:], cw[:, :, bass.ds(four * EU, EU)]))
            if l == 3:
                b1f = b1[:].rearrange("p e c -> p (e c)")
                sem["cwcur"].by(dve.tensor_copy(b1Cur[:].rearrange("p a b -> p (a b)"),
                                                b1f[:, bass.ds(four * EU * 4, EU * 4)]))
            wait(act, "cwcur")
            wait(dve, "cwcur")
            outf = Fout[:].rearrange("p e k d -> p (e k d)")
            todo = []
            n_act = 0

            def finish(unit, k, b, hbuf, ready):
                bank = MX[:, unit % 2, :]
                wait(pe, "hready", ready)
                wait(pe, "yread", QT * (unit - 1))
                for t in range(QT):
                    for j in range(nk):
                        ins = pe.matmul(bank[:, t * P:(t + 1) * P], hT[0:fs, hbuf, j, t * P:(t + 1) * P],
                                        outf[0:fs, bass.ds(four * EU * 4 * D + (k * 4 + j) * D, D)],
                                        start=j == 0, stop=j == nk - 1)
                sem["y"].by(ins)
                wait(dve, "y")
                for t in range(QT):
                    tt = b * QT + t
                    wait(dve, "yread", sem["yread"].n - QT)
                    sem["yread"].by(dve.scalar_tensor_tensor(yacc[:, tt, :], bank[:, t * P:(t + 1) * P],
                                                             cwCur[:, tt, k:k + 1], yacc[:, tt, :], ALU.mult, ALU.add))

            unit = 0
            for k in range(EU):
                wait(pe, *staged[k])
                for b in range(NQB):
                    hb = unit % 2
                    tok = slice(b * CH, (b + 1) * CH)
                    for j in range(nk):
                        sides = ([j, nk + j] if gated else [j])
                        q = n_act % 2
                        wait(pe, "hready", n_act - 1)
                        for s, col in enumerate(sides):
                            ins = pe.matmul(S[0:fs, 2 * q + s, :], FinCur[:, k % 2, col * fs:(col + 1) * fs], xnT[:, tok],
                                            start=True, stop=True)
                        sem["h"].by(ins)
                        wait(act, "h")
                        wait(act, "y", unit - 1)
                        bias = b1Cur[:, k, j:j + 1] if l == 3 else 0.0
                        if gated:
                            wait(act, "hready", n_act - 1)
                            sem["hact"].by(act.activation(gA[0:fs, q, :], S[0:fs, 2 * q, :], f["act"], bias=bias))
                            wait(dve, "hact")
                            if l == 3:
                                ins = dve.scalar_tensor_tensor(hT[0:fs, hb, j, :], S[0:fs, 2 * q + 1, :],
                                                               b1Cur[:, k, nk + j:nk + j + 1], gA[0:fs, q, :],
                                                               ALU.add, ALU.mult)
                            else:
                                ins = dve.tensor_tensor(hT[0:fs, hb, j, :], S[0:fs, 2 * q + 1, :], gA[0:fs, q, :],
                                                        ALU.mult)
                        else:
                            ins = act.activation(hT[0:fs, hb, j, :], S[0:fs, 2 * q, :], f["act"])
                        sem["hready"].by(ins)
                        n_act += 1
                    if todo:
                        todo.pop(0)()
                    ready = sem["hready"].n

                    def later(unit=unit, k=k, b=b, hb=hb, ready=ready):
                        finish(unit, k, b, hb, ready)
                    todo.append(later)
                    unit += 1
                w_read[k] = sem["h"].n
                if k + 2 < EU:
                    staged[k + 2] = stage(k + 2)
            for x in todo:
                x()
            barrier()

        def ffn(l):
            f = FFN[l]
            if l < 3:
                get_stack(KA, l + 1, 0, d_stack[l + 1])
            for eng in (pe, dve, act, pool):
                loaded(eng, d_ffn[l])
            state = xs
            v_turns = [lambda j=j: project_v(l + 1, j, j % 2) for j in range(VJ if l < 3 else 0)]
            for x in v_turns[:V_NORM]:
                x()
            norm(xn, xs, 1e-5)
            if l == 1:
                state = zs
                step(after(dve).tensor_copy(zs[:], xn[:]))
            for loop in range(f["loops"]):
                if l == 1:
                    norm(xn, zs, 1e-6, centre=False, weight=normw)
                transpose_tiles(xnT, lambda t: xn[:, t, :])
                route(l, v_turns[V_NORM:] if loop == 0 else [])
                if l == 3:
                    for b in range(NQB):
                        after(pe)
                        for t in range(QT):
                            last = pe.transpose(S[0:E, b, t * P:(t + 1) * P], cw[:, b * QT + t, :], ident[:])
                        step(last)
                        step(after(dve).tensor_copy(cwT[:, b * CH:(b + 1) * CH], S[0:E, b, :]))
                    for b in range(NQB):
                        after(pe)
                        for t in range(QT):
                            tt = b * QT + t
                            last = pe.matmul(S[:, b, t * P:(t + 1) * P], cwT[:, tt * P:(tt + 1) * P], b2[:],
                                             start=True, stop=True)
                        step(last)
                        step(after(dve).tensor_copy(yacc[:, b * QT:(b + 1) * QT, :],
                                                    S[:, b, :].rearrange("p (t d) -> p t d", d=D)))
                else:
                    step(after(dve).memset(yacc[:], 0.0))
                barrier()
                with nc.Fori(0, E // EU) as four:
                    experts(l, four)
                step(after(dve).tensor_tensor(state[:], state[:], yacc[:], ALU.add))
            if l == 1:
                step(after(dve).tensor_tensor(xs[:], xs[:], zs[:], ALU.add))

        zeros = sb("zeros", [P, P])
        pool.memset(zeros[:], 0.0)
        for eng in (pe, act, dve, pool):
            loaded(eng, d_const)
        barrier()
        for l in range(4):
            load_ffn(l)
            if l < 3:
                load_attn(l + 1)
            attention(l)
            ffn(l)
            barrier()
        d_out.by(sp.dma_start(out.rearrange("(t p) d -> p t d", p=P), xs[:]), 16)
        loaded(sp, d_out)


def _layout(i):
    import numpy as np
    f = np.float32
    a = {}
    a["x"] = np.asarray(i["x"])[0]
    a["mask"] = np.asarray(i["mask_BxSxS2_bf1"])[0].view(np.uint8)
    a["maskT"] = a["mask"].T
    a["ctxT"] = np.asarray(i["ctx_1024"])[0].T

    names = [("L0_xattn_", "Wq bq Wk bk Wv bv Wo bo"), ("L1_xattn_", "W_q b_q W_k b_k W_v b_v W_out b_out"),
             ("L2_xattn_", "Wq - Wk - Wv - Wo -"), ("L3_xattn_", "W_q b_q W_k b_k W_v b_v W_o b_o")]

    def stack(w):
        s = np.zeros((D, NG, HG, 4, DH), f)
        s[:, :, :, 0:3, :] = w.reshape(D, NG, HG, 1, DH)
        return s.reshape(D, NG, P)

    for l, (pre, ns) in enumerate(names):
        wq, bq, wk, bk, wv, bv, wo, bo = (np.zeros(D, f) if n == "-" else np.asarray(i[pre + n]) for n in ns.split())
        a[f"Wq{l}"], a[f"Wk{l}"] = stack(wq.T), wk.T
        a[f"Wv{l}"], a[f"Wo{l}"] = wv.T, wo.T
        a[f"bq{l}"] = stack(np.broadcast_to(bq, (D, D)))[0].T
        a[f"bk{l}"] = bk.reshape(D, 1)
        a[f"bvo{l}"] = np.stack([bv, bo])
    n = {k: np.asarray(v) for k, v in i.items() if "ffn" in k}
    a["Fin0"] = n["L0_ffn_c_fc"].transpose(1, 0, 2)
    a["Fout0"] = n["L0_ffn_c_proj"].reshape(E, 2, 96, D).transpose(2, 0, 1, 3)
    a["Wg0"] = n["L0_ffn_w_gate"]
    a["Fin1"] = np.concatenate([n["L1_ffn_w1"], n["L1_ffn_w3"]], axis=2).transpose(1, 0, 2)
    a["Fout1"] = n["L1_ffn_w2"].reshape(E, 2, P, D).transpose(2, 0, 1, 3)
    a["Wg1"] = n["L1_ffn_router_w"]
    a["normw"] = n["L1_ffn_norm_w"]
    a["Fin2"] = n["L2_ffn_expert_up"].transpose(2, 0, 1)
    a["Fout2"] = n["L2_ffn_expert_down"].transpose(0, 2, 1).reshape(E, 4, P, D).transpose(2, 0, 1, 3)
    a["Wg2"] = n["L2_ffn_router_w"]
    a["rb2"] = np.stack([n["L2_ffn_router_b"], np.zeros(E, f)])
    a["Fin3"] = n["L3_ffn_Wl1"].transpose(1, 0, 2)
    a["Fout3"] = n["L3_ffn_Wl2"].reshape(E, 2, P, D).transpose(2, 0, 1, 3)
    a["Wg3"] = n["L3_ffn_Wr"].T
    a["rb3"] = np.stack([n["L3_ffn_br"], n["L3_ffn_biases_N"]])
    a["b1"] = n["L3_ffn_bl1"].reshape(E, 4, P).transpose(2, 0, 1)
    a["b2"] = n["L3_ffn_bl2"]
    r = np.arange(P) % ROWS
    lo_q = (r >= DH) & (r < 2 * DH)
    a["cst"] = np.stack([np.where(lo_q, -1, 1), lo_q, M_SCALE * (r == M_ROW)], 1).astype(f)
    a["ident"] = np.eye(P, dtype=f)
    a["upper"] = np.triu(np.ones((P, P), f), 1)
    a["ones"] = np.ones((P, P), f)
    a["iota"] = np.arange(E, dtype=f)
    return {k: np.ascontiguousarray(v) for k, v in a.items()}


def kernel(**inputs):
    import concourse.bacc as _bacc
    from concourse import mybir as _mybir
    from concourse.bass_utils import run_bass_kernel_spmd as _run

    nc = _bacc.Bacc("TRN2", target_bir_lowering=False, num_devices=1)
    arrays, args = {}, {}
    for name, a in _layout(inputs).items():
        arrays[f"in_{name}"] = a
        args[name] = nc.dram_tensor(f"in_{name}", a.shape, _mybir.dt.from_np(a.dtype), kind="ExternalInput").ap()
    out = nc.dram_tensor("out_x", (T, D), _mybir.dt.from_np(arrays["in_x"].dtype), kind="ExternalOutput").ap()
    build(nc, args, out)
    r = _run(nc, [arrays], core_ids=[0])
    return r.results[0]["out_x"].reshape(1, T, D)
```
